# Optimizing a Trainium2 kernel written in Bass

```python
import numpy as np
import jax
import jax.numpy as jnp

def _softmax(x, axis=-1):
    return jax.nn.softmax(x, axis=axis)

def _gelu(x):
    return jax.nn.gelu(x, approximate=True)

def _silu(x):
    return jax.nn.silu(x)

def _sigmoid(x):
    return jax.nn.sigmoid(x)

def _layernorm(x, axis=-1, eps=1e-05):
    m = jnp.mean(x, axis=axis, keepdims=True)
    v = jnp.var(x, axis=axis, keepdims=True)
    return (x - m) / jnp.sqrt(v + eps)

def _scatter_add(tgt, idx, src, axis=0):
    return tgt.at[idx].add(src)

def _segment_sum(src, seg, n):
    return jax.ops.segment_sum(src, seg, n)
kernel_name = 'mk_adj_preln_d4_adj_r2_0ea17b'

def setup_inputs(seed: int=0):
    np.random.seed(seed)
    _w = jnp.asarray

    def _rec_inputs():
        import jax
        import jax.numpy as jnp
        _gk = jax.random.key(seed)
        x = -0.0002928 + 1 * jax.random.normal(jax.random.fold_in(_gk, 1), (8, 1024, 128), jnp.float32)
        _a = jax.random.bernoulli(jax.random.fold_in(_gk, 2), 0.00195312, (8, 1024, 1024))
        _a = jnp.logical_or(_a, jnp.swapaxes(_a, -1, -2))
        _a = jnp.logical_or(_a, jnp.eye(1024, dtype=bool))
        _af = _a.astype(jnp.float32)
        _af = _af * jax.random.uniform(jax.random.fold_in(_gk, 3), (8, 1024, 1024), jnp.float32, 0.05, 1)
        adj = _af
        _nm = jnp.ones((8, 1024), dtype=bool)
        nodemask = jnp.where(_nm, 1.0, 0.0).astype(jnp.float32)
        return (x, adj, nodemask)
    x, adj, nodemask = _rec_inputs()

    def _L0_gnn_setup():
        import jax, jax.numpy as jnp
        import numpy as np
        B, N, D, H = (8, 1024, 128, 512)
        RMS_EPS = 1e-06

        def _rmsnorm(h, w, eps=RMS_EPS):
            var = jnp.mean(jnp.square(h), axis=-1, keepdims=True)
            return h * jax.lax.rsqrt(var + eps) * w
        key = jax.random.key(seed)
        ks = jax.random.split(key, 5)
        x = jax.random.normal(ks[0], (B, N, D), dtype=jnp.float32)
        adjacency = jax.random.uniform(ks[1], (B, N, N), dtype=jnp.float32)
        epsilon = jnp.zeros((), dtype=jnp.float32)
        W1 = jax.random.normal(ks[2], (D, H), dtype=jnp.float32) * (1.0 / np.sqrt(D))
        b1 = jnp.zeros((H,), dtype=jnp.float32)
        rms_weight = jnp.ones((H,), dtype=jnp.float32)
        W2 = jax.random.normal(ks[3], (H, D), dtype=jnp.float32) * (1.0 / np.sqrt(H))
        b2 = jnp.zeros((D,), dtype=jnp.float32)
        return {'x': x, 'adjacency': adjacency, 'epsilon': epsilon, 'W1': W1, 'b1': b1, 'rms_weight': rms_weight, 'W2': W2, 'b2': b2}
    _L0_gnn_all = _L0_gnn_setup()
    _L0_gnn_in = {k: v for k, v in _L0_gnn_all.items() if k in ('epsilon', 'W1', 'b1', 'rms_weight', 'W2', 'b2')}
    del _L0_gnn_all

    def _L1_gnn_setup():
        import jax, jax.numpy as jnp
        import numpy as np
        B, K, H = (32, 512, 128)
        LN_EPS = 1e-05

        def layer_norm(x, gamma, beta):
            mu = jnp.mean(x, axis=-1, keepdims=True)
            var = jnp.mean(jnp.square(x - mu), axis=-1, keepdims=True)
            return (x - mu) * jax.lax.rsqrt(var + LN_EPS) * gamma + beta
        key = jax.random.key(seed)
        k1, k2, k3, k4 = jax.random.split(key, 4)
        x = jax.random.normal(k1, (B, K, H), dtype=jnp.float32)
        adj = jax.random.uniform(k2, (B, K, K), dtype=jnp.float32)
        s = 1.0 / np.sqrt(H)
        W_rel = jax.random.normal(k3, (H, H), dtype=jnp.float32) * s
        b_rel = jnp.zeros((H,), dtype=jnp.float32)
        W_root = jax.random.normal(k4, (H, H), dtype=jnp.float32) * s
        ln_gamma = jnp.ones((H,), dtype=jnp.float32)
        ln_beta = jnp.zeros((H,), dtype=jnp.float32)
        return {'x': x, 'adj': adj, 'W_rel': W_rel, 'b_rel': b_rel, 'W_root': W_root, 'ln_gamma': ln_gamma, 'ln_beta': ln_beta}
    _L1_gnn_all = _L1_gnn_setup()
    _L1_gnn_in = {k: v for k, v in _L1_gnn_all.items() if k in ('W_rel', 'b_rel', 'W_root', 'ln_gamma', 'ln_beta')}
    del _L1_gnn_all

    def _L2_gnn_setup():
        import jax, jax.numpy as jnp
        import numpy as np
        key = jax.random.key(seed)
        k1, k2, k3, k4 = jax.random.split(key, 4)
        B, N, F_in, F_out = (8, 1024, 128, 128)
        x = jax.random.normal(k1, (B, N, F_in), dtype=jnp.float32)
        adj = jax.random.uniform(k2, (B, N, N), dtype=jnp.float32)
        stdv = 1.0 / np.sqrt(F_out)
        weight = jax.random.uniform(k3, (F_in, F_out), dtype=jnp.float32, minval=-stdv, maxval=stdv)
        bias = jax.random.uniform(k4, (F_out,), dtype=jnp.float32, minval=-stdv, maxval=stdv)
        return {'x': x, 'adj': adj, 'weight': weight, 'bias': bias}
    _L2_gnn_all = _L2_gnn_setup()
    _L2_gnn_in = {k: v for k, v in _L2_gnn_all.items() if k in ('weight', 'bias')}
    del _L2_gnn_all

    def _L3_gnn_setup():
        import jax, jax.numpy as jnp
        import numpy as np
        B, N, D, C, L = (64, 256, 128, 128, 5)
        EDGE_P = 0.02

        def _gru_cell(m, h, w_ih, w_hh, b_ih, b_hh):
            gi = m @ w_ih.T + b_ih
            gh = h @ w_hh.T + b_hh
            i_r, i_z, i_n = jnp.split(gi, 3, axis=-1)
            h_r, h_z, h_n = jnp.split(gh, 3, axis=-1)
            r = jax.nn.sigmoid(i_r + h_r)
            z = jax.nn.sigmoid(i_z + h_z)
            n = jnp.tanh(i_n + r * h_n)
            return (1.0 - z) * n + z * h
        key = jax.random.key(seed)
        ks = jax.random.split(key, 8)
        x = jax.random.normal(ks[0], (B, N, D), dtype=jnp.float32)
        adj = (jax.random.uniform(ks[1], (B, N, N)) < EDGE_P).astype(jnp.float32)
        mask = jnp.ones((B, N), dtype=jnp.float32)
        s = 1.0 / np.sqrt(C).astype(np.float32)
        weight = jax.random.uniform(ks[2], (L, C, C), minval=-s, maxval=s, dtype=jnp.float32)
        w_ih = jax.random.uniform(ks[3], (3 * C, C), minval=-s, maxval=s, dtype=jnp.float32)
        w_hh = jax.random.uniform(ks[4], (3 * C, C), minval=-s, maxval=s, dtype=jnp.float32)
        b_ih = jax.random.uniform(ks[5], (3 * C,), minval=-s, maxval=s, dtype=jnp.float32)
        b_hh = jax.random.uniform(ks[6], (3 * C,), minval=-s, maxval=s, dtype=jnp.float32)
        return dict(x=x, adj=adj, mask=mask, weight=weight, w_ih=w_ih, w_hh=w_hh, b_ih=b_ih, b_hh=b_hh)
    _L3_gnn_all = _L3_gnn_setup()
    _L3_gnn_in = {k: v for k, v in _L3_gnn_all.items() if k in ('weight', 'w_ih', 'w_hh', 'b_ih', 'b_hh')}
    del _L3_gnn_all
    return {'x': x, 'adj': adj, 'nodemask': nodemask, 'L0_gnn_epsilon': _L0_gnn_in['epsilon'], 'L0_gnn_W1': _L0_gnn_in['W1'], 'L0_gnn_b1': _L0_gnn_in['b1'], 'L0_gnn_rms_weight': _L0_gnn_in['rms_weight'], 'L0_gnn_W2': _L0_gnn_in['W2'], 'L0_gnn_b2': _L0_gnn_in['b2'], 'L1_gnn_W_rel': _L1_gnn_in['W_rel'], 'L1_gnn_b_rel': _L1_gnn_in['b_rel'], 'L1_gnn_W_root': _L1_gnn_in['W_root'], 'L1_gnn_ln_gamma': _L1_gnn_in['ln_gamma'], 'L1_gnn_ln_beta': _L1_gnn_in['ln_beta'], 'L2_gnn_weight': _L2_gnn_in['weight'], 'L2_gnn_bias': _L2_gnn_in['bias'], 'L3_gnn_weight': _L3_gnn_in['weight'], 'L3_gnn_w_ih': _L3_gnn_in['w_ih'], 'L3_gnn_w_hh': _L3_gnn_in['w_hh'], 'L3_gnn_b_ih': _L3_gnn_in['b_ih'], 'L3_gnn_b_hh': _L3_gnn_in['b_hh']}

def reference(x, adj, nodemask, L0_gnn_epsilon, L0_gnn_W1, L0_gnn_b1, L0_gnn_rms_weight, L0_gnn_W2, L0_gnn_b2, L1_gnn_W_rel, L1_gnn_b_rel, L1_gnn_W_root, L1_gnn_ln_gamma, L1_gnn_ln_beta, L2_gnn_weight, L2_gnn_bias, L3_gnn_weight, L3_gnn_w_ih, L3_gnn_w_hh, L3_gnn_b_ih, L3_gnn_b_hh):
    import jax
    import jax.numpy as jnp

    def _L0_gnn_ref(x, adjacency, epsilon, W1, b1, rms_weight, W2, b2):
        import jax, jax.numpy as jnp
        import numpy as np
        B, N, D, H = (8, 1024, 128, 512)
        RMS_EPS = 1e-06

        def _rmsnorm(h, w, eps=RMS_EPS):
            var = jnp.mean(jnp.square(h), axis=-1, keepdims=True)
            return h * jax.lax.rsqrt(var + eps) * w
        neighbor_sum = jnp.einsum('bnm,bmd->bnd', adjacency, x)
        agg = epsilon * x + neighbor_sum
        h = jnp.einsum('bnd,dh->bnh', agg, W1) + b1
        h = jax.nn.silu(_rmsnorm(h, rms_weight))
        out = jnp.einsum('bnh,hd->bnd', h, W2) + b2
        return out

    def _L1_gnn_ref(x, adj, W_rel, b_rel, W_root, ln_gamma, ln_beta):
        import jax, jax.numpy as jnp
        import numpy as np
        B, K, H = (32, 512, 128)
        LN_EPS = 1e-05

        def layer_norm(x, gamma, beta):
            mu = jnp.mean(x, axis=-1, keepdims=True)
            var = jnp.mean(jnp.square(x - mu), axis=-1, keepdims=True)
            return (x - mu) * jax.lax.rsqrt(var + LN_EPS) * gamma + beta
        h = layer_norm(x, ln_gamma, ln_beta)
        agg = jnp.einsum('bij,bjh->bih', adj, h)
        conv = jnp.einsum('bkh,ho->bko', agg, W_rel) + b_rel + jnp.einsum('bkh,ho->bko', h, W_root)
        return x + jax.nn.relu(conv)

    def _L2_gnn_ref(x, adj, weight, bias):
        import jax, jax.numpy as jnp
        import numpy as np
        support = jnp.einsum('bni,io->bno', x, weight)
        out = jnp.einsum('bnm,bmo->bno', adj, support)
        return out + bias

    def _L3_gnn_ref(x, adj, mask, weight, w_ih, w_hh, b_ih, b_hh):
        import jax, jax.numpy as jnp
        import numpy as np
        B, N, D, C, L = (64, 256, 128, 128, 5)
        EDGE_P = 0.02

        def _gru_cell(m, h, w_ih, w_hh, b_ih, b_hh):
            gi = m @ w_ih.T + b_ih
            gh = h @ w_hh.T + b_hh
            i_r, i_z, i_n = jnp.split(gi, 3, axis=-1)
            h_r, h_z, h_n = jnp.split(gh, 3, axis=-1)
            r = jax.nn.sigmoid(i_r + h_r)
            z = jax.nn.sigmoid(i_z + h_z)
            n = jnp.tanh(i_n + r * h_n)
            return (1.0 - z) * n + z * h
        A = (adj != 0).astype(x.dtype)
        h = x
        for l in range(weight.shape[0]):
            m = jnp.einsum('bnd,de->bne', h, weight[l])
            agg = jnp.einsum('bij,bid->bjd', A, m)
            h = _gru_cell(agg, h, w_ih, w_hh, b_ih, b_hh)
        return h * mask[..., None]
    h = jnp.maximum(_layernorm(x, axis=-1), 0.0)
    x = x + _L0_gnn_ref(h, adj, L0_gnn_epsilon, L0_gnn_W1, L0_gnn_b1, L0_gnn_rms_weight, L0_gnn_W2, L0_gnn_b2)
    h = jnp.maximum(_layernorm(x, axis=-1), 0.0)
    x = x + _L1_gnn_ref(h, adj, L1_gnn_W_rel, L1_gnn_b_rel, L1_gnn_W_root, L1_gnn_ln_gamma, L1_gnn_ln_beta)
    h = jnp.maximum(_layernorm(x, axis=-1), 0.0)
    x = x + _L2_gnn_ref(h, adj, L2_gnn_weight, L2_gnn_bias)
    h = jnp.maximum(_layernorm(x, axis=-1), 0.0)
    x = x + _L3_gnn_ref(h, adj, nodemask, L3_gnn_weight, L3_gnn_w_ih, L3_gnn_w_hh, L3_gnn_b_ih, L3_gnn_b_hh)
    return x

_drawn_inputs = setup_inputs


def setup_inputs(seed=0):
    import zlib

    import numpy as np

    out = dict(_drawn_inputs(seed))
    spreads = {'L0_gnn_b1': (0.0, 0.1),
     'L0_gnn_rms_weight': (1.0, 0.2),
     'L0_gnn_b2': (0.0, 0.1),
     'L1_gnn_b_rel': (0.0, 0.1),
     'L1_gnn_ln_gamma': (1.0, 0.2),
     'L1_gnn_ln_beta': (0.0, 0.1)}
    factors = {'L2_gnn_bias': 3.123, 'L3_gnn_b_hh': 5.157}
    for name, (base, spread) in spreads.items():
        noise = np.random.default_rng([zlib.crc32(name.encode()), seed]).standard_normal(out[name].shape)
        drawn = base * np.exp(spread * noise) if base else spread * noise
        out[name] = jnp.asarray(drawn.astype(out[name].dtype))
    for name, factor in factors.items():
        out[name] = (out[name] * factor).astype(out[name].dtype)
    return out
```

```python
from contextlib import ExitStack

import concourse.bass as bass
from concourse import mybir

ALU = mybir.AluOpType
ACT = mybir.ActivationFunctionType
F32 = mybir.dt.float32
F32R = mybir.dt.float32r
F16 = mybir.dt.float16
BF16 = mybir.dt.bfloat16
F8 = mybir.dt.float8e4
U16 = mybir.dt.uint16

P = 128
EPS_LN = 1e-5
EPS_RMS = 1e-6
HSCALE = 1024.0


def schedule(has_gru, has_front):
    slots = {
        "start": [("A", 0), ("A", 1)],
        "a0": [("A", 2)],
        "b0": [("A", 3), ("A", 4)],
        "c0": [("A", 5), ("N0", 0), ("A", 6)],
        "a1": [("A", 7)],
        "b1": [("M", 0)],
        "c1": [("M", 1)],
        "a2": [("W", 0), ("W", 1)],
        "b2": [("W", 2)],
        "c2": [("W", 3)],
        "a3": [("W", 4), ("N1", 0)],
        "b3": [("M", 2)],
        "c3": [("M", 3)],
        "a4": [("C", 0), ("N2", 0)],
        "b4": [("M", 4)],
        "c4": [("M", 5), ("C", 1), ("N3", 0)],
    }
    order = []

    def slot(name):
        if has_front:
            order.extend(slots[name])

    def gru(*stages):
        if has_gru:
            order.extend(stages)

    slot("start")
    gru(("S", (0, 0)), ("S", (0, 1)))
    for s in range(5):
        gru(("E", s))
        slot(f"a{s}")
        gru(("G", s))
        slot(f"b{s}")
        if has_front or s == 4:
            gru(("T", (s, 0)), ("T", (s, 1)))
            if s == 4:
                gru(("MASK", 0))
            slot(f"c{s}")
            if s < 4:
                gru(("S", (s + 1, 0)), ("S", (s + 1, 1)))
        else:
            gru(("T", (s, 0)), ("S", (s + 1, 0)), ("T", (s, 1)), ("S", (s + 1, 1)))
    return order


def adj_preln_kernel(nc, t_in, out):
    x, adj, nodemask = t_in["x"], t_in["adj"], t_in["nodemask"]
    B, N, D = x.shape
    H = t_in["W1"].shape[1]
    L = t_in["WlT"].shape[0]
    KT = N // P
    HB = H // P
    CH = 512
    NC = N // CH
    TC = CH // P
    G3 = 3 * D
    assert D == P and NC == 2 and L == 5 and HB == 4 and KT == 8

    ctx = ExitStack()
    with ctx:
        def sb(name, shape, dt):
            return ctx.enter_context(nc.sbuf_tensor(name, shape, dt))

        def pb(name):
            return ctx.enter_context(nc.psum_tensor(name, [P, CH], F32))

        per = {}

        def sem(name, per_graph):
            s = ctx.enter_context(nc.semaphore(name))
            per[s.name] = per_graph
            return s

        def nth(signal, g, k):
            value = g * per[signal.name] + k
            return max(value, 0) if isinstance(value, int) else value

        def held(eng, value):
            return value if isinstance(value, int) else eng.to_reg(value)

        adjT_hi = sb("adjT_hi", [P, KT, N], F32R)
        adjT_lo = sb("adjT_lo", [P, KT, N], F32R)
        edges_next = sb("edges_next", [P, KT, N], F8)
        edges = sb("edges", [P, KT, N], F8)
        adj_rows = sb("adj_rows", [P, 2, N], F32)
        xf = sb("xf", [P, KT, D], F32)
        xg = sb("xg", [P, KT, D], F32)
        fn_hi = sb("fn_hi", [P, KT, D], F32R)
        fn_lo = sb("fn_lo", [P, KT, D], F32R)
        gn_hi = sb("gn_hi", [P, KT, D], F16)
        gn_lo = sb("gn_lo", [P, KT, D], F16)
        h = sb("h", [P, N], F32)
        h_hi = sb("h_hi", [P, N], F32R)
        h_lo = sb("h_lo", [P, N], F32R)
        s_hi = sb("s_hi", [P, N], F32R)
        s_lo = sb("s_lo", [P, N], F32R)
        r_t = sb("r_t", [P, NC, CH], F32)
        z_t = sb("z_t", [P, NC, CH], F32)
        n_t = sb("n_t", [P, NC, CH], F32)
        ag_hi = sb("ag_hi", [P, N], F32R)
        ag_lo = sb("ag_lo", [P, N], F32R)
        y_hi = sb("y_hi", [P, N], F32R)
        y_lo = sb("y_lo", [P, N], F32R)
        ew = sb("ew", [P, 3 * N], F32)
        mlp_outT = sb("mlp_outT", [P, 2 * P], F32)
        junk = sb("junk", [P, H], BF16)

        NB = H + HB * D + 3 * D + G3
        w_hi = sb("w_hi", [P, NB + L * G3], F32R)
        w_lo = sb("w_lo", [P, NB + L * G3], F32R)
        b1_b = sb("b1_b", [P, H], F32)
        rms_b = sb("rms_b", [P, H], F32)
        gamma_b = sb("gamma_b", [P, D], F32)
        beta_b = sb("beta_b", [P, D], F32)
        ident = sb("ident", [P, P], F32)
        cols = sb("cols", [P, 16], F32)
        mask = sb("mask", [P, KT], F32)
        stats = sb("stats", [P, KT, 6], F32)
        meanvar = sb("meanvar", [P, KT, 2], F32)
        vareps = sb("vareps", [P, KT], F32)
        rstd = sb("rstd", [P, KT], F32)
        ssq = sb("ssq", [P, KT], F32)
        mseps = sb("mseps", [P, KT], F32)
        rrms = sb("rrms", [P, KT], F32)
        neghalf = sb("neghalf", [P, KT], F32)

        c1 = ew[:, 0:N].rearrange("p (t d) -> p t d", d=D)
        c2 = ew[:, N:2 * N].rearrange("p (t d) -> p t d", d=D)
        conv_outT = ew[:, 0:N]
        hid = ew[:, 0:4 * H].rearrange("p (b n) -> p b n", b=4)
        sig = ew[:, 4 * H:6 * H].rearrange("p (b n) -> p b n", b=2)
        ehT = ew[:, N:2 * N]

        raw = ew
        R_IH, R_L = NB, NB + G3
        O_W1, O_W2, O_REL = 0, H, H + HB * D
        O_ROOT, O_L2 = O_REL + D, O_REL + 2 * D
        O_HH, O_G = O_REL + 3 * D, NB

        def w(o, n=P):
            return w_hi[:, o:o + n], w_lo[:, o:o + n]

        B2, BREL, BL2, BIR, BIZ, BIN, BHR, BHZ, BHN, EPSC, BR, BZ = range(12)

        def col(k):
            return cols[:, k:k + 1]

        bank = [pb(f"bank{i}") for i in range(8)]
        P_R, P_Z, P_HN, P_IN = bank[0], bank[1], bank[2], bank[3]
        P_S = bank[4:6]
        P_T = bank[0:2]
        P_F = bank[6:8]

        w_loaded = sem("w_loaded", 0)
        ident_done = sem("ident_done", 0)
        w_hi_done = sem("w_hi_done", 0)
        w_lo_done = sem("w_lo_done", 0)
        fold_done = sem("fold_done", 0)
        bias_done = sem("bias_done", 0)
        setup_done = sem("setup_done", 0)

        adj_in = [sem(f"adj_in{i}", 16 * KT // 2) for i in range(2)]
        x_in = sem("x_in", 16)
        mask_in = sem("mask_in", 16)
        out_stored = sem("out_stored", 32)
        adj_turned = sem("adj_turned", 2 * KT)
        adj_hi_done = sem("adj_hi_done", 2 * KT)
        adj_lo_done = sem("adj_lo_done", 2 * KT)
        edges_done = sem("edges_done", KT)
        edges_taken = sem("edges_taken", 1)

        bn_done = sem("bn_done", 5)
        meanvar_done = sem("meanvar_done", 5)
        vareps_done = sem("vareps_done", 5)
        rstd_done = sem("rstd_done", 5)
        centred = sem("centred", 5)
        normed = sem("normed", 5)
        scaled = sem("scaled", 1)
        affine = sem("affine", 1)
        relud = sem("relud", 1)
        skip_added = sem("skip_added", 1)
        fn_hi_done = sem("fn_hi_done", 3)
        fn_lo_done = sem("fn_lo_done", 3)
        fn_turned = sem("fn_turned", 4)
        ehT_done = sem("ehT_done", 2)
        hT_hi_done = sem("hT_hi_done", 2)
        hT_lo_done = sem("hT_lo_done", 2)
        ag_done = sem("ag_done", 6)
        ag_summed = sem("ag_summed", 2)
        ag_hi_done = sem("ag_hi_done", 6)
        ag_lo_done = sem("ag_lo_done", 6)
        hid_done = sem("hid_done", KT)
        hid_biased = sem("hid_biased", KT)
        squared = sem("squared", KT)
        mseps_done = sem("mseps_done", KT // 2)
        rrms_done = sem("rrms_done", KT // 2)
        hid_normed = sem("hid_normed", KT)
        sig_done = sem("sig_done", KT)
        silu_done = sem("silu_done", KT)
        hid_turned = sem("hid_turned", KT)
        hidT_hi_done = sem("hidT_hi_done", KT)
        hidT_lo_done = sem("hidT_lo_done", KT)
        mlp_done = sem("mlp_done", KT // 2)
        mlp_biased = sem("mlp_biased", KT // 2)
        mlp_turned = sem("mlp_turned", KT // 2)
        x1_done = sem("x1_done", KT // 2)
        conv_done = sem("conv_done", 4)
        conv_biased = sem("conv_biased", 4)
        conv_turned = sem("conv_turned", 4)
        x2_done = sem("x2_done", 2)
        x3_done = sem("x3_done", 2)
        hr_done = sem("hr_done", 2)
        h0_turned = sem("h0_turned", 2)

        gn_hi_done = sem("gn_hi_done", 2 * L)
        gn_lo_done = sem("gn_lo_done", 2 * L)
        h_new = sem("h_new", 2 * L + 2)
        h_hi_done = sem("h_hi_done", 2 * L)
        h_lo_done = sem("h_lo_done", 2 * L)
        s_done = sem("s_done", 2 * L)
        s_hi_done = sem("s_hi_done", 2 * L)
        s_lo_done = sem("s_lo_done", 2 * L)
        gate_done = sem("gate_done", 8 * L)
        rz_done = sem("rz_done", 4 * L)
        rhn_done = sem("rhn_done", 2 * L)
        narg_done = sem("narg_done", 2 * L)
        n_done = sem("n_done", 2 * L)
        diff_done = sem("diff_done", 2 * L)
        zdiff_done = sem("zdiff_done", 2 * L)
        h_turned = sem("h_turned", 2 * L)
        out_done = sem("out_done", 2)

        block = ctx.enter_context(nc.Block())

        def run(eng, stages):
            def go(order, g, f):
                for name, k in order:
                    if name in stages:
                        stages[name](g if name in GRU_STAGES else f, k)

            go(schedule(False, True), None, 0)
            go(schedule(True, True), 0, 1)
            with eng.Fori(1, B - 1) as g:
                go(schedule(True, True), g, g + 1)
            go(schedule(True, False), B - 1, None)

        GRU_STAGES = ("S", "E", "G", "T", "MASK")

        @block.sync
        def _(sp):
            def load_w(dst, src):
                sp.dma_start(dst, src).then_inc(w_loaded, 16)

            load_w(raw[:, O_W1:O_W1 + H], t_in["W1"])
            load_w(raw[:, O_W2:O_W2 + HB * D].rearrange("p (b d) -> p b d", b=HB),
                   t_in["W2"].rearrange("(b p) d -> p b d", p=P))
            load_w(raw[:, O_REL:O_REL + D], t_in["W_rel"])
            load_w(raw[:, O_ROOT:O_ROOT + D], t_in["W_root"])
            load_w(raw[:, O_L2:O_L2 + D], t_in["W_l2"])
            load_w(raw[:, O_HH:O_HH + G3], t_in["whhT"])
            load_w(raw[:, R_IH:R_IH + G3], t_in["wihT"])
            load_w(raw[:, R_L:R_L + L * D].rearrange("p (l d) -> p l d", l=L),
                   t_in["WlT"].rearrange("l e d -> e l d"))
            for dst, name in ((b1_b, "b1"), (rms_b, "rms"), (gamma_b, "gamma"), (beta_b, "beta")):
                load_w(dst[:, :], t_in[name].partition_broadcast(P))
            load_w(col(EPSC), t_in["epsilon"].partition_broadcast(P))
            for k, name in ((B2, "b2"), (BREL, "b_rel"), (BL2, "b_l2")):
                load_w(col(k), t_in[name].rearrange("(p a) -> p a", a=1))
            load_w(cols[:, BIR:BIR + 3], t_in["b_ih"])
            load_w(cols[:, BHR:BHR + 3], t_in["b_hh"])

            def A(f, t):
                if t == 0:
                    count = held(sp, nth(x3_done, f, 0))
                    sp.wait_ge(setup_done, 1)
                    sp.wait_ge(x3_done, count)
                    sp.dma_start(xf[:, :, :], x[f, :, :].rearrange("(t p) d -> p t d", p=P)
                                 ).then_inc(x_in, 16)
                count = held(sp, nth(adj_turned, f, 2 * t - 2))
                sp.wait_ge(setup_done, 1)
                sp.wait_ge(adj_turned, count)
                count = held(sp, nth(edges_done, f, t - 1))
                sp.wait_ge(setup_done, 1)
                sp.wait_ge(edges_done, count)
                sp.dma_start(adj_rows[:, t % 2, :], adj[f, t * P:(t + 1) * P, :]
                             ).then_inc(adj_in[t % 2], 16)

            def G(g, s):
                if s == 0:
                    count = held(sp, nth(out_done, g, 0))
                    sp.wait_ge(setup_done, 1)
                    sp.wait_ge(out_done, count)
                    sp.dma_start(mask[:, :], nodemask[g, :, :]).then_inc(mask_in, 16)

            def MASK(g, k):
                for c in range(NC):
                    count = held(sp, nth(out_done, g, c + 1))
                    sp.wait_ge(setup_done, 1)
                    sp.wait_ge(out_done, count)
                    sp.dma_start(out[g, c * CH:(c + 1) * CH, :].rearrange("(t p) d -> p t d", p=P),
                                 xg[:, c * TC:(c + 1) * TC, :]).then_inc(out_stored, 16)

            run(sp, {"A": A, "G": G, "MASK": MASK})
            sp.wait_ge(out_stored, nth(out_stored, B, 0))

        N_WLOADS = 16 * 18

        @block.tensor
        def _(pe):
            def product(ps, weight, moving, start, stop):
                (wh, wl), (mh, ml) = weight, moving
                pe.matmul(ps, wh, mh, start=start, stop=False)
                pe.matmul(ps, wl, mh, start=False, stop=False)
                return pe.matmul(ps, wh, ml, start=False, stop=stop)

            def turn(ps, tiles):
                for j, tile in enumerate(tiles):
                    last = pe.transpose(ps[:, j * P:(j + 1) * P], tile, ident[:, :])
                return last

            def A(f, t):
                pe.wait_ge(adj_in[t % 2], nth(adj_in[t % 2], f, 16 * (t // 2 + 1)))
                for q in range(2):
                    if t == 0:
                        pe.wait_ge(h_new, nth(h_new, f, q + 1 - per[h_new.name]))
                    if t == 6:
                        pe.wait_ge(ehT_done, nth(ehT_done, f, q + 1))
                    pe.wait_ge(adj_lo_done, nth(adj_lo_done, f, 2 * t + q - 1))
                    turn(P_F[q], [adj_rows[:, t % 2, (4 * q + j) * P:(4 * q + j + 1) * P]
                                  for j in range(4)]).then_inc(adj_turned, 1)

            def N0(f, k):
                pe.wait_ge(normed, nth(normed, f, 1))
                for c in range(NC):
                    pe.wait_ge(adj_lo_done, nth(adj_lo_done, f, 2 * 5 + c + 1))
                    turn(P_F[c], [c1[:, c * TC + j, :] for j in range(TC)]).then_inc(fn_turned, 1)

            def M(f, k):
                layer, c = k // 2, k % 2
                pe.wait_ge(fn_lo_done, nth(fn_lo_done, f, layer + 1))
                if layer == 0:
                    pe.wait_ge(adj_lo_done, nth(adj_lo_done, f, 2 * KT))
                    pe.wait_ge(ehT_done, nth(ehT_done, f, c + 1))
                if layer == 1:
                    pe.wait_ge(hT_lo_done, nth(hT_lo_done, f, c + 1))
                if layer == 2:
                    pe.wait_ge(x2_done, nth(x2_done, f, c + 1))
                cs = slice(c * CH, (c + 1) * CH)
                for m in range(KT):
                    last = product(P_F[c][:, :], (fn_hi[:, m, :], fn_lo[:, m, :]),
                                   (adjT_hi[:, m, cs], adjT_lo[:, m, cs]),
                                   start=(m == 0), stop=(m == KT - 1))
                last.then_inc(ag_done, 1)

            def hidden(f, t):
                pe.wait_ge(ag_lo_done, nth(ag_lo_done, f, t // TC + 1))
                pe.wait_ge(hid_biased, nth(hid_biased, f, t))
                ns = slice(t * P, (t + 1) * P)
                product(P_F[0][:, :], (ag_hi[:, ns], ag_lo[:, ns]), w(O_W1, H), True, True
                        ).then_inc(hid_done, 1)

            def W(f, u):
                if u < 4:
                    if u >= 2:
                        pe.wait_ge(mlp_biased, nth(mlp_biased, f, u - 1))
                    if u == 0:
                        pe.wait_ge(ag_lo_done, nth(ag_lo_done, f, 2))
                    hidden(f, 2 * u)
                    hidden(f, 2 * u + 1)
                if u >= 2:
                    pe.wait_ge(mlp_biased, nth(mlp_biased, f, u - 1))
                    pe.wait_ge(hidT_lo_done, nth(hidT_lo_done, f, 2 * u - 2))
                    turn(P_F[1], [mlp_outT[:, j * P:(j + 1) * P] for j in range(2)]
                         ).then_inc(mlp_turned, 1)
                if u >= 1:
                    v = u - 1
                    for t in (2 * v, 2 * v + 1):
                        pe.wait_ge(silu_done, nth(silu_done, f, t + 1))
                        pe.wait_ge(hidT_lo_done, nth(hidT_lo_done, f, t))
                        if t == 2 * v and v > 0:
                            pe.wait_ge(x1_done, nth(x1_done, f, v))
                        turn(P_F[1], [hid[:, t % 4, b * P:(b + 1) * P] for b in range(HB)]
                             ).then_inc(hid_turned, 1)
                    pe.wait_ge(hidT_lo_done, nth(hidT_lo_done, f, 2 * v + 2))
                    pe.wait_ge(hid_biased, nth(hid_biased, f, min(2 * u + 2, KT)))
                    for b in range(HB):
                        last = product(P_F[0][:, 0:2 * P], w(O_W2 + b * D),
                                       (y_hi[:, b * 2 * P:(b + 1) * 2 * P],
                                        y_lo[:, b * 2 * P:(b + 1) * 2 * P]),
                                       start=(b == 0), stop=(b == HB - 1))
                    last.then_inc(mlp_done, 1)
                if u == 4:
                    pe.wait_ge(mlp_biased, nth(mlp_biased, f, 4))
                    turn(P_F[1], [mlp_outT[:, j * P:(j + 1) * P] for j in range(2)]
                         ).then_inc(mlp_turned, 1)

            def N1(f, k):
                pe.wait_ge(affine, nth(affine, f, 1))
                pe.wait_ge(x1_done, nth(x1_done, f, 4))
                for c in range(NC):
                    turn(P_F[c], [c2[:, c * TC + j, :] for j in range(TC)]).then_inc(fn_turned, 1)

            def C(f, k):
                for c in range(NC):
                    cs = slice(c * CH, (c + 1) * CH)
                    pe.wait_ge(ag_lo_done, nth(ag_lo_done, f, 2 * k + 3 + c))
                    agg = (ag_hi[:, cs], ag_lo[:, cs])
                    if k == 0:
                        product(P_F[c][:, :], w(O_REL), agg, True, False)
                        last = product(P_F[c][:, :], w(O_ROOT), (y_hi[:, cs], y_lo[:, cs]), False, True)
                    else:
                        last = product(P_F[c][:, :], w(O_L2), agg, True, True)
                    last.then_inc(conv_done, 1)
                for c in range(NC):
                    pe.wait_ge(conv_biased, nth(conv_biased, f, 2 * k + c + 1))
                    turn(P_F[c], [conv_outT[:, (c * TC + j) * P:(c * TC + j + 1) * P]
                                  for j in range(TC)]).then_inc(conv_turned, 1)

            def N3(f, k):
                pe.wait_ge(x3_done, nth(x3_done, f, 2))
                for c in range(NC):
                    pe.wait_ge(hr_done, nth(hr_done, f, c + 1))
                    turn(P_F[c], [c1[:, c * TC + j, :] for j in range(TC)]).then_inc(h0_turned, 1)

            def S(g, k):
                s, half = k
                if s == 0 and half == 0:
                    count = held(pe, nth(edges_taken, g, 1))
                    pe.wait_ge(setup_done, 1)
                    pe.wait_ge(edges_taken, count)
                count = held(pe, nth(gn_lo_done, g, 2 * s + half + 1))
                pe.wait_ge(setup_done, 1)
                pe.wait_ge(gn_lo_done, count)
                for c in range(NC):
                    for m in range(half * TC, (half + 1) * TC):
                        for part in (gn_hi, gn_lo):
                            last = pe.matmul(P_S[c][:, :], part[:, m, :],
                                             edges[:, m, c * CH:(c + 1) * CH],
                                             start=(m == 0 and part is gn_hi),
                                             stop=(m == KT - 1 and part is gn_lo))
                    if half == 1:
                        last.then_inc(s_done, 1)

            def G(g, s):
                for c in range(NC):
                    i = 2 * s + c
                    cs = slice(c * CH, (c + 1) * CH)
                    state = (h_hi[:, cs], h_lo[:, cs])
                    agg = (s_hi[:, cs], s_lo[:, cs])
                    ih, hh = O_G + s * G3, O_HH
                    pe.wait_ge(h_lo_done, nth(h_lo_done, g, i + 1))
                    pe.wait_ge(rhn_done, nth(rhn_done, g, i))
                    product(P_HN[:, :], w(hh + 2 * D), state, True, True).then_inc(gate_done, 1)
                    if i == 0:
                        pe.wait_ge(out_done, nth(out_done, g, 0))
                    pe.wait_ge(rz_done, nth(rz_done, g, 2 * i - 1))
                    product(P_R[:, :], w(hh), state, True, False)
                    pe.wait_ge(s_lo_done, nth(s_lo_done, g, i + 1))
                    product(P_R[:, :], w(ih), agg, False, True).then_inc(gate_done, 1)
                    pe.wait_ge(rz_done, nth(rz_done, g, 2 * i))
                    product(P_Z[:, :], w(hh + D), state, True, False)
                    product(P_Z[:, :], w(ih + D), agg, False, True).then_inc(gate_done, 1)
                    pe.wait_ge(narg_done, nth(narg_done, g, i))
                    product(P_IN[:, :], w(ih + 2 * D), agg, True, True).then_inc(gate_done, 1)

            def T(g, k):
                s, c = k
                pe.wait_ge(h_new, nth(h_new, g, 2 + 2 * s + c + 1))
                pe.wait_ge(rz_done, nth(rz_done, g, 2 * (2 * s + 1) + 1 + c))
                turn(P_T[c], [h[:, (c * TC + j) * P:(c * TC + j + 1) * P] for j in range(TC)]
                     ).then_inc(h_turned, 1)

            pe.wait_ge(w_loaded, N_WLOADS)
            pe.wait_ge(ident_done, 3)
            for l in range(L):
                pe.matmul(bank[l][:, 0:G3], raw[:, R_L + l * D:R_L + (l + 1) * D],
                          raw[:, R_IH:R_IH + G3], start=True, stop=True).then_inc(fold_done, 1)
            pe.wait_ge(w_lo_done, L + 1)
            run(pe, {"A": A, "N0": N0, "M": M, "W": W, "N1": N1, "C": C, "N3": N3,
                     "S": S, "G": G, "T": T})

        @block.scalar
        def _(act):
            def A(f, t):
                for q in range(2):
                    act.wait_ge(adj_turned, nth(adj_turned, f, 2 * t + q + 1))
                    act.activation(adjT_hi[:, 4 * q:4 * q + 4, t * P:(t + 1) * P],
                                   P_F[q][:, :].rearrange("p (j n) -> p j n", j=4), ACT.Copy
                                   ).then_inc(adj_hi_done, 1)

            def N0(f, k):
                act.wait_ge(normed, nth(normed, f, 1))
                act.activation(fn_hi[:, :, :], c1, ACT.Relu).then_inc(fn_hi_done, 1)

            def M(f, k):
                layer, c = k // 2, k % 2
                cs = slice(c * CH, (c + 1) * CH)
                if layer == 0:
                    act.wait_ge(ag_summed, nth(ag_summed, f, c + 1))
                    src = ehT[:, cs]
                else:
                    act.wait_ge(ag_done, nth(ag_done, f, k + 1))
                    src = P_F[c][:, :]
                act.activation(ag_hi[:, cs], src, ACT.Copy).then_inc(ag_hi_done, 1)

            def W(f, u):
                if u >= 1:
                    for t in (2 * u - 2, 2 * u - 1):
                        act.wait_ge(hid_normed, nth(hid_normed, f, t + 1))
                        act.wait_ge(silu_done, nth(silu_done, f, t - 1))
                        act.activation(sig[:, t % 2, :], hid[:, t % 4, :], ACT.Sigmoid
                                       ).then_inc(sig_done, 1)
                if u < 4:
                    for t in (2 * u, 2 * u + 1):
                        act.wait_ge(hid_biased, nth(hid_biased, f, t + 1))
                        act.wait_ge(squared, nth(squared, f, t))
                        act.activation(junk[:, :], hid[:, t % 4, :], ACT.Square,
                                       accum_out=ssq[:, t:t + 1]).then_inc(squared, 1)

                def bias_out(v):
                    act.wait_ge(mlp_done, nth(mlp_done, f, v + 1))
                    act.wait_ge(mlp_turned, nth(mlp_turned, f, v))
                    act.activation(mlp_outT[:, :], P_F[0][:, 0:2 * P], ACT.Identity, bias=col(B2)
                                   ).then_inc(mlp_biased, 1)

                if u >= 1:
                    for t in (2 * u - 2, 2 * u - 1):
                        act.wait_ge(hid_turned, nth(hid_turned, f, t + 1))
                        act.activation(
                            y_hi[:, :].rearrange("p (b n) -> p b n", b=HB)[:, :, (t % 2) * P:(t % 2 + 1) * P],
                            P_F[1][:, :].rearrange("p (b n) -> p b n", b=HB), ACT.Copy
                        ).then_inc(hidT_hi_done, 1)
                    bias_out(u - 1)

            def N1(f, k):
                act.wait_ge(normed, nth(normed, f, 2))
                act.activation(c1, c1, ACT.Relu).then_inc(relud, 1)
                act.wait_ge(affine, nth(affine, f, 1))
                act.activation(fn_hi[:, :, :], c2, ACT.Copy).then_inc(fn_hi_done, 1)
                for c in range(NC):
                    cs = slice(c * CH, (c + 1) * CH)
                    act.wait_ge(fn_turned, nth(fn_turned, f, 2 + c + 1))
                    act.activation(y_hi[:, cs], P_F[c][:, :], ACT.Copy).then_inc(hT_hi_done, 1)

            def C(f, k):
                if k == 0:
                    act.wait_ge(skip_added, nth(skip_added, f, 1))
                for c in range(NC):
                    act.wait_ge(conv_done, nth(conv_done, f, 2 * k + c + 1))
                    act.activation(conv_outT[:, c * CH:(c + 1) * CH], P_F[c][:, :],
                                   ACT.Relu if k == 0 else ACT.Identity,
                                   bias=col(BREL if k == 0 else BL2)).then_inc(conv_biased, 1)

            def N2(f, k):
                act.wait_ge(normed, nth(normed, f, 4))
                act.activation(fn_hi[:, :, :], c1, ACT.Relu).then_inc(fn_hi_done, 1)

            def N3(f, k):
                act.wait_ge(normed, nth(normed, f, 5))
                for c in range(NC):
                    part = c1[:, c * TC:(c + 1) * TC, :]
                    act.activation(part, part, ACT.Relu, scale=HSCALE).then_inc(hr_done, 1)
                for c in range(NC):
                    ts = slice(c * TC, (c + 1) * TC)
                    act.wait_ge(hr_done, nth(hr_done, f, c + 1))
                    act.wait_ge(s_done, nth(s_done, f, 0))
                    act.activation(gn_hi[:, ts, :], c1[:, ts, :], ACT.Copy).then_inc(gn_hi_done, 1)
                for c in range(NC):
                    cs = slice(c * CH, (c + 1) * CH)
                    act.wait_ge(h0_turned, nth(h0_turned, f, c + 1))
                    act.wait_ge(h_turned, nth(h_turned, f, 0))
                    act.activation(h[:, cs], P_F[c][:, :], ACT.Copy, scale=1.0 / HSCALE
                                   ).then_inc(h_new, 1)

            def E(g, s):
                for c in range(NC):
                    act.wait_ge(s_done, nth(s_done, g, 2 * s + c + 1))
                    act.activation(s_hi[:, c * CH:(c + 1) * CH], P_S[c][:, :], ACT.Copy,
                                   scale=1.0 / HSCALE).then_inc(s_hi_done, 1)

            def G(g, s):
                for c in range(NC):
                    i = 2 * s + c
                    act.wait_ge(gate_done, nth(gate_done, g, 4 * i + 2))
                    act.activation(r_t[:, c, :], P_R[:, :], ACT.Sigmoid, bias=col(BR)
                                   ).then_inc(rz_done, 1)
                    act.wait_ge(gate_done, nth(gate_done, g, 4 * i + 3))
                    act.activation(z_t[:, c, :], P_Z[:, :], ACT.Sigmoid, bias=col(BZ)
                                   ).then_inc(rz_done, 1)
                    act.wait_ge(narg_done, nth(narg_done, g, i + 1))
                    act.activation(n_t[:, c, :], n_t[:, c, :], ACT.Tanh, bias=col(BIN)
                                   ).then_inc(n_done, 1)

            def T(g, k):
                s, c = k
                if s < L - 1:
                    act.wait_ge(h_turned, nth(h_turned, g, 2 * s + c + 1))
                    act.activation(gn_hi[:, c * TC:(c + 1) * TC, :],
                                   P_T[c][:, :].rearrange("p (t d) -> p t d", d=D), ACT.Copy,
                                   scale=HSCALE).then_inc(gn_hi_done, 1)

            act.wait_ge(w_loaded, N_WLOADS)
            act.activation(w_hi[:, 0:NB], raw[:, 0:NB], ACT.Copy).then_inc(w_hi_done, 1)
            for l in range(L):
                act.wait_ge(fold_done, l + 1)
                act.activation(w_hi[:, O_G + l * G3:O_G + (l + 1) * G3], bank[l][:, 0:G3], ACT.Copy
                               ).then_inc(w_hi_done, 1)
            act.wait_ge(bias_done, 1)
            run(act, {"A": A, "N0": N0, "M": M, "W": W, "N1": N1, "C": C, "N2": N2, "N3": N3,
                      "E": E, "G": G, "T": T})

        @block.vector
        def _(dve):
            def over_features(v):
                return v.to_broadcast([P, KT, D])

            def norm(f, j, src, dst):
                for t in range(KT):
                    last = dve.bn_stats(stats[:, t, :], src[:, t, :])
                last.then_inc(bn_done, 1)
                count = held(dve, nth(bn_done, f, j + 1))
                dve.wait_ge(setup_done, 1)
                dve.wait_ge(bn_done, count)
                for t in range(KT):
                    last = dve.bn_aggr(meanvar[:, t, :], stats[:, t, :])
                last.then_inc(meanvar_done, 1)
                dve.wait_ge(meanvar_done, nth(meanvar_done, f, j + 1))
                dve.wait_ge(rstd_done, nth(rstd_done, f, j))
                dve.tensor_scalar(vareps[:, :].unsqueeze(2), meanvar[:, :, 1:2], EPS_LN, None, ALU.add
                                  ).then_inc(vareps_done, 1)
                dve.tensor_tensor(dst, src, over_features(meanvar[:, :, 0:1]), ALU.subtract
                                  ).then_inc(centred, 1)
                dve.wait_ge(centred, nth(centred, f, j + 1))
                dve.wait_ge(rstd_done, nth(rstd_done, f, j + 1))
                dve.tensor_tensor(dst, dst, over_features(rstd[:, :].unsqueeze(2)), ALU.mult
                                  ).then_inc(normed, 1)

            def A(f, t):
                count = held(dve, nth(adj_in[t % 2], f, 16 * (t // 2 + 1)))
                dve.wait_ge(setup_done, 1)
                dve.wait_ge(adj_in[t % 2], count)
                count = held(dve, nth(edges_taken, f, 0))
                dve.wait_ge(setup_done, 1)
                dve.wait_ge(edges_taken, count)
                dve.tensor_scalar(edges_next[:, t, :], adj_rows[:, t % 2, :], 0.0, None, ALU.not_equal,
                                  saturate=False
                                  ).then_inc(edges_done, 1)
                for q in range(2):
                    dve.wait_ge(adj_hi_done, nth(adj_hi_done, f, 2 * t + q + 1))
                    js, ns = slice(4 * q, 4 * q + 4), slice(t * P, (t + 1) * P)
                    dve.tensor_tensor(adjT_lo[:, js, ns],
                                      P_F[q][:, :].rearrange("p (j n) -> p j n", j=4),
                                      adjT_hi[:, js, ns].bitcast(F32), ALU.subtract
                                      ).then_inc(adj_lo_done, 1)

            def N0(f, k):
                dve.wait_ge(x_in, nth(x_in, f, 16))
                norm(f, 0, xf[:, :, :], c1)
                dve.wait_ge(fn_hi_done, nth(fn_hi_done, f, 1))
                dve.scalar_tensor_tensor(fn_lo[:, :, :], c1, 0.0, fn_hi[:, :, :].bitcast(F32),
                                         ALU.max, ALU.subtract).then_inc(fn_lo_done, 1)
                for c in range(NC):
                    dve.wait_ge(fn_turned, nth(fn_turned, f, c + 1))
                    dve.tensor_scalar(ehT[:, c * CH:(c + 1) * CH], P_F[c][:, :], 0.0, col(EPSC),
                                      ALU.max, ALU.mult).then_inc(ehT_done, 1)

            def M(f, k):
                layer, c = k // 2, k % 2
                cs = slice(c * CH, (c + 1) * CH)
                if layer == 0:
                    dve.wait_ge(ag_done, nth(ag_done, f, c + 1))
                    dve.tensor_tensor(ehT[:, cs], P_F[c][:, :], ehT[:, cs], ALU.add
                                      ).then_inc(ag_summed, 1)
                    src = ehT[:, cs]
                else:
                    src = P_F[c][:, :]
                dve.wait_ge(ag_hi_done, nth(ag_hi_done, f, k + 1))
                dve.tensor_tensor(ag_lo[:, cs], src, ag_hi[:, cs].bitcast(F32), ALU.subtract
                                  ).then_inc(ag_lo_done, 1)

            def W(f, u):
                if u >= 1:
                    v = u - 1
                    dve.wait_ge(rrms_done, nth(rrms_done, f, v + 1))
                    for t in (2 * v, 2 * v + 1):
                        dve.scalar_tensor_tensor(hid[:, t % 4, :], hid[:, t % 4, :], rrms[:, t:t + 1],
                                                 rms_b[:, :], ALU.mult, ALU.mult
                                                 ).then_inc(hid_normed, 1)
                if u < 4:
                    for t in (2 * u, 2 * u + 1):
                        dve.wait_ge(hid_done, nth(hid_done, f, t + 1))
                        dve.wait_ge(hid_turned, nth(hid_turned, f, t - 3))
                        dve.tensor_tensor(hid[:, t % 4, :], P_F[0][:, :], b1_b[:, :], ALU.add
                                          ).then_inc(hid_biased, 1)
                    dve.wait_ge(squared, nth(squared, f, 2 * u + 2))
                    dve.tensor_scalar(mseps[:, 2 * u:2 * u + 2], ssq[:, 2 * u:2 * u + 2], 1.0 / H,
                                      EPS_RMS, ALU.mult, ALU.add).then_inc(mseps_done, 1)

                def add_out(v):
                    dve.wait_ge(mlp_turned, nth(mlp_turned, f, v + 1))
                    part = xf[:, 2 * v:2 * v + 2, :]
                    dve.tensor_tensor(part, P_F[1][:, 0:2 * P].rearrange("p (t d) -> p t d", d=D),
                                      part, ALU.add).then_inc(x1_done, 1)

                if u >= 2:
                    add_out(u - 2)
                if u >= 1:
                    for t in (2 * u - 2, 2 * u - 1):
                        dve.wait_ge(hidT_hi_done, nth(hidT_hi_done, f, t + 1))
                        bs = slice((t % 2) * P, (t % 2 + 1) * P)
                        dve.tensor_tensor(
                            y_lo[:, :].rearrange("p (b n) -> p b n", b=HB)[:, :, bs],
                            P_F[1][:, :].rearrange("p (b n) -> p b n", b=HB),
                            y_hi[:, :].bitcast(F32).rearrange("p (b n) -> p b n", b=HB)[:, :, bs],
                            ALU.subtract).then_inc(hidT_lo_done, 1)
                if u == 4:
                    add_out(3)

            def N1(f, k):
                dve.wait_ge(x1_done, nth(x1_done, f, 4))
                norm(f, 1, xf[:, :, :], c1)
                dve.wait_ge(relud, nth(relud, f, 1))
                norm(f, 2, c1, c2)
                dve.wait_ge(normed, nth(normed, f, 3))
                dve.tensor_tensor(c2, c2, gamma_b[:, :].unsqueeze(1).to_broadcast([P, KT, D]), ALU.mult
                                  ).then_inc(scaled, 1)
                dve.wait_ge(scaled, nth(scaled, f, 1))
                dve.tensor_tensor(c2, c2, beta_b[:, :].unsqueeze(1).to_broadcast([P, KT, D]), ALU.add
                                  ).then_inc(affine, 1)
                dve.wait_ge(fn_hi_done, nth(fn_hi_done, f, 2))
                dve.wait_ge(affine, nth(affine, f, 1))
                dve.tensor_tensor(fn_lo[:, :, :], c2, fn_hi[:, :, :].bitcast(F32), ALU.subtract
                                  ).then_inc(fn_lo_done, 1)
                for c in range(NC):
                    cs = slice(c * CH, (c + 1) * CH)
                    dve.wait_ge(hT_hi_done, nth(hT_hi_done, f, c + 1))
                    dve.tensor_tensor(y_lo[:, cs], P_F[c][:, :], y_hi[:, cs].bitcast(F32), ALU.subtract
                                      ).then_inc(hT_lo_done, 1)

            def C(f, k):
                for c in range(NC):
                    ts = slice(c * TC, (c + 1) * TC)
                    dve.wait_ge(conv_turned, nth(conv_turned, f, 2 * k + c + 1))
                    src = P_F[c][:, :].rearrange("p (t d) -> p t d", d=D)
                    if k == 0:
                        dve.wait_ge(skip_added, nth(skip_added, f, 1))
                        dve.tensor_tensor(xf[:, ts, :], src, xf[:, ts, :], ALU.add
                                          ).then_inc(x2_done, 1)
                    else:
                        dve.wait_ge(out_stored, nth(out_stored, f, 0))
                        dve.tensor_tensor(xg[:, ts, :], src, xf[:, ts, :], ALU.add
                                          ).then_inc(x3_done, 1)

            def N2(f, k):
                dve.wait_ge(x2_done, nth(x2_done, f, 2))
                norm(f, 3, xf[:, :, :], c1)
                dve.wait_ge(fn_hi_done, nth(fn_hi_done, f, 3))
                dve.scalar_tensor_tensor(fn_lo[:, :, :], c1, 0.0, fn_hi[:, :, :].bitcast(F32),
                                         ALU.max, ALU.subtract).then_inc(fn_lo_done, 1)

            def take_edges(f):
                dve.wait_ge(s_done, nth(s_done, f, 0))
                dve.wait_ge(edges_done, nth(edges_done, f, KT))
                dve.tensor_copy(edges[:, :, :].bitcast(U16), edges_next[:, :, :].bitcast(U16)
                                ).then_inc(edges_taken, 1)

            def N3(f, k):
                take_edges(f)
                dve.wait_ge(x3_done, nth(x3_done, f, 2))
                norm(f, 4, xg[:, :, :], c1)
                for c in range(NC):
                    ts = slice(c * TC, (c + 1) * TC)
                    dve.wait_ge(gn_hi_done, nth(gn_hi_done, f, c + 1))
                    dve.tensor_tensor(gn_lo[:, ts, :], c1[:, ts, :], gn_hi[:, ts, :], ALU.subtract
                                      ).then_inc(gn_lo_done, 1)
                for c in range(NC):
                    state_lo(f, c)

            def state_lo(g, i):
                cs = slice((i % 2) * CH, (i % 2 + 1) * CH)
                dve.wait_ge(h_hi_done, nth(h_hi_done, g, i + 1))
                dve.tensor_tensor(h_lo[:, cs], h[:, cs], h_hi[:, cs].bitcast(F32), ALU.subtract
                                  ).then_inc(h_lo_done, 1)

            def E(g, s):
                for c in range(NC):
                    cs = slice(c * CH, (c + 1) * CH)
                    dve.wait_ge(s_hi_done, nth(s_hi_done, g, 2 * s + c + 1))
                    dve.scalar_tensor_tensor(s_lo[:, cs], P_S[c][:, :], 1.0 / HSCALE,
                                             s_hi[:, cs].bitcast(F32), ALU.mult, ALU.subtract
                                             ).then_inc(s_lo_done, 1)

            def G(g, s):
                for c in range(NC):
                    i = 2 * s + c
                    cs = slice(c * CH, (c + 1) * CH)
                    dve.wait_ge(gate_done, nth(gate_done, g, 4 * i + 1))
                    dve.wait_ge(rz_done, nth(rz_done, g, 2 * i + 1))
                    dve.scalar_tensor_tensor(n_t[:, c, :], P_HN[:, :], col(BHN), r_t[:, c, :],
                                             ALU.add, ALU.mult).then_inc(rhn_done, 1)
                    dve.wait_ge(gate_done, nth(gate_done, g, 4 * i + 4))
                    dve.wait_ge(rhn_done, nth(rhn_done, g, i + 1))
                    dve.tensor_tensor(n_t[:, c, :], P_IN[:, :], n_t[:, c, :], ALU.add
                                      ).then_inc(narg_done, 1)
                    dve.wait_ge(n_done, nth(n_done, g, i + 1))
                    dve.tensor_tensor(r_t[:, c, :], h[:, cs], n_t[:, c, :], ALU.subtract
                                      ).then_inc(diff_done, 1)
                    dve.wait_ge(diff_done, nth(diff_done, g, i + 1))
                    dve.wait_ge(rz_done, nth(rz_done, g, 2 * i + 2))
                    dve.tensor_tensor(r_t[:, c, :], r_t[:, c, :], z_t[:, c, :], ALU.mult
                                      ).then_inc(zdiff_done, 1)
                    dve.wait_ge(zdiff_done, nth(zdiff_done, g, i + 1))
                    dve.tensor_tensor(h[:, cs], r_t[:, c, :], n_t[:, c, :], ALU.add
                                      ).then_inc(h_new, 1)
                if s < L - 1:
                    for c in range(NC):
                        state_lo(g, 2 * (s + 1) + c)

            def T(g, k):
                s, c = k
                ts = slice(c * TC, (c + 1) * TC)
                if s < L - 1:
                    dve.wait_ge(gn_hi_done, nth(gn_hi_done, g, 2 * (s + 1) + c + 1))
                    dve.scalar_tensor_tensor(gn_lo[:, ts, :],
                                             P_T[c][:, :].rearrange("p (t d) -> p t d", d=D), HSCALE,
                                             gn_hi[:, ts, :], ALU.mult, ALU.subtract
                                             ).then_inc(gn_lo_done, 1)
                else:
                    dve.wait_ge(h_turned, nth(h_turned, g, 2 * s + c + 1))
                    dve.wait_ge(mask_in, nth(mask_in, g, 16))
                    for j in range(TC):
                        t = c * TC + j
                        last = dve.scalar_tensor_tensor(xg[:, t, :], P_T[c][:, j * P:(j + 1) * P],
                                                        mask[:, t:t + 1], xg[:, t, :],
                                                        ALU.mult, ALU.add)
                    last.then_inc(out_done, 1)

            dve.memset(neghalf[:, :], -0.5).then_inc(ident_done, 1)
            dve.wait_ge(w_loaded, N_WLOADS)
            dve.tensor_tensor(cols[:, BR:BR + 2], cols[:, BIR:BIR + 2], cols[:, BHR:BHR + 2], ALU.add
                              ).then_inc(bias_done, 1)
            dve.memset(ssq[:, :], 0.0).then_inc(setup_done, 1)
            dve.wait_ge(w_hi_done, 1)
            dve.tensor_tensor(w_lo[:, 0:NB], raw[:, 0:NB], w_hi[:, 0:NB].bitcast(F32), ALU.subtract
                              ).then_inc(w_lo_done, 1)
            for l in range(L):
                part = slice(O_G + l * G3, O_G + (l + 1) * G3)
                dve.wait_ge(w_hi_done, l + 2)
                dve.tensor_tensor(w_lo[:, part], bank[l][:, 0:G3], w_hi[:, part].bitcast(F32),
                                  ALU.subtract).then_inc(w_lo_done, 1)
            run(dve, {"A": A, "N0": N0, "M": M, "W": W, "N1": N1, "C": C, "N2": N2, "N3": N3,
                      "E": E, "G": G, "T": T})

        @block.gpsimd
        def _(pool):
            def norm_power(f, j):
                pool.wait_ge(vareps_done, nth(vareps_done, f, j + 1))
                pool.wait_ge(normed, nth(normed, f, j))
                pool.tensor_tensor(rstd[:, :], vareps[:, :], neghalf[:, :], ALU.pow
                                   ).then_inc(rstd_done, 1)

            def N0(f, k):
                norm_power(f, 0)

            def N1(f, k):
                norm_power(f, 1)
                pool.wait_ge(relud, nth(relud, f, 1))
                norm_power(f, 2)
                pool.tensor_tensor(xf[:, :, :], xf[:, :, :], c1, ALU.add).then_inc(skip_added, 1)

            def N2(f, k):
                norm_power(f, 3)

            def N3(f, k):
                norm_power(f, 4)
                for c in range(NC):
                    state_hi(f, c)

            def W(f, u):
                if u >= 1:
                    for t in (2 * u - 2, 2 * u - 1):
                        pool.wait_ge(sig_done, nth(sig_done, f, t + 1))
                        pool.tensor_tensor(hid[:, t % 4, :], hid[:, t % 4, :], sig[:, t % 2, :],
                                           ALU.mult).then_inc(silu_done, 1)
                if u < 4:
                    pool.wait_ge(mseps_done, nth(mseps_done, f, u + 1))
                    pool.tensor_tensor(rrms[:, 2 * u:2 * u + 2], mseps[:, 2 * u:2 * u + 2],
                                       neghalf[:, 0:2], ALU.pow).then_inc(rrms_done, 1)

            def state_hi(g, i):
                cs = slice((i % 2) * CH, (i % 2 + 1) * CH)
                count = held(pool, nth(h_new, g, i + 1))
                pool.wait_ge(setup_done, 1)
                pool.wait_ge(h_new, count)
                pool.tensor_scalar(h_hi[:, cs], h[:, cs], 1.0, 0.0, ALU.mult, ALU.add
                                   ).then_inc(h_hi_done, 1)

            def G(g, s):
                if s < L - 1:
                    for c in range(NC):
                        state_hi(g, 2 * (s + 1) + c)

            pool.memset(ident[:, :], 0.0).then_inc(ident_done, 1)
            pool.wait_ge(ident_done, 2)
            pool.affine_select(out=ident[:, :], in_=ident[:, :], compare_op=ALU.not_equal, fill=1.0,
                               base=0, pattern=[[-1, P]], channel_multiplier=1
                               ).then_inc(ident_done, 1)
            run(pool, {"N0": N0, "N1": N1, "N2": N2, "N3": N3, "W": W, "G": G})


def kernel(**inputs):
    import numpy as _np
    import concourse.bacc as _bacc
    from concourse import mybir as _mybir
    from concourse.bass_utils import run_bass_kernel_spmd as _run

    c = _np.ascontiguousarray
    laid = {
        "x": c(inputs["x"]), "adj": c(inputs["adj"]), "nodemask": c(_np.transpose(inputs["nodemask"].reshape(8, 8, 128), (0, 2, 1))),
        "epsilon": c(inputs["L0_gnn_epsilon"]).reshape(1),
        "W1": c(inputs["L0_gnn_W1"]), "b1": c(inputs["L0_gnn_b1"]), "rms": c(inputs["L0_gnn_rms_weight"]),
        "W2": c(inputs["L0_gnn_W2"]), "b2": c(inputs["L0_gnn_b2"]),
        "W_rel": c(inputs["L1_gnn_W_rel"]), "b_rel": c(inputs["L1_gnn_b_rel"]),
        "W_root": c(inputs["L1_gnn_W_root"]), "gamma": c(inputs["L1_gnn_ln_gamma"]),
        "beta": c(inputs["L1_gnn_ln_beta"]),
        "W_l2": c(inputs["L2_gnn_weight"]), "b_l2": c(inputs["L2_gnn_bias"]),
        "WlT": c(_np.transpose(inputs["L3_gnn_weight"], (0, 2, 1))),
        "wihT": c(_np.transpose(inputs["L3_gnn_w_ih"])), "whhT": c(_np.transpose(inputs["L3_gnn_w_hh"])),
        "b_ih": c(_np.transpose(inputs["L3_gnn_b_ih"].reshape(3, 128))),
        "b_hh": c(_np.transpose(inputs["L3_gnn_b_hh"].reshape(3, 128))),
    }
    nc = _bacc.Bacc("TRN2", target_bir_lowering=False, num_devices=1)
    arrays, args = {}, {}
    for name, a in laid.items():
        arrays[f"in_{name}_dram"] = a
        args[name] = nc.dram_tensor(f"in_{name}_dram", a.shape, _mybir.dt.from_np(a.dtype),
                                    kind="ExternalInput").ap()
    out = nc.dram_tensor("out_0_dram", laid["x"].shape, _mybir.dt.from_np(laid["x"].dtype),
                         kind="ExternalOutput").ap()
    adj_preln_kernel(nc, args, out)
    r = _run(nc, [arrays], core_ids=[0])
    return r.results[0]["out_0_dram"]
```

```python
from contextlib import ExitStack

import concourse.bass as bass
from concourse import mybir

ALU = mybir.AluOpType
ACT = mybir.ActivationFunctionType
F32 = mybir.dt.float32
F32R = mybir.dt.float32r
F16 = mybir.dt.float16
BF16 = mybir.dt.bfloat16
F8 = mybir.dt.float8e4
U16 = mybir.dt.uint16

P = 128
EPS_LN = 1e-5
EPS_RMS = 1e-6
HSCALE = 1024.0


AHEAD = {"gru": 0, "front": 1, "next": 2}
HEAD_ADJ = 4

SP_ORDER = [
    "front adj 4, front adj 5, front adj 6, front adj 7, gru mask, next adj 0, gru store 0",
    "gru store 1, next adj 1, next adj 2, next x, next adj 3",
]

PE_ORDER = [
    "gru agg 0 0, front adj 4 0, front adj 4 1, gru agg 0 1, front adj 5 0, front adj 5 1",
    "gru hn 0 0, gru r 0 0, front adj 6 0, front adj 6 1, gru in 0 0, gru z 0 0",
    "front adj 7 0, gru hn 0 1, gru r 0 1, front adj 7 1, gru in 0 1, gru hT 0 0, gru z 0 1",
    "front turn0 0, gru agg 1 0, front turn0 1, front gather 0 0, gru hT 0 1, gru hn 1 0",
    "front gather 0 1, gru agg 1 1, front mlp1 0, gru r 1 0, front mlp1 1, gru in 1 0",
    "gru z 1 0, front mlp1 2, gru hn 1 1, gru r 1 1, front mlp1 3, gru in 1 1, front hidT 0",
    "gru z 1 1, gru hT 1 0, front hidT 1, front mlp1 4, front mlp1 5, gru agg 2 0",
    "front mlp2 0, front hidT 2, gru hT 1 1, gru hn 2 0, front hidT 3, front mlp1 6",
    "gru agg 2 1, front mlp1 7, front mlpT 0, gru r 2 0, front mlp2 1, front hidT 4",
    "gru in 2 0, gru z 2 0, front hidT 5, gru hn 2 1, gru r 2 1, front mlpT 1, front mlp2 2",
    "front hidT 6, gru in 2 1, gru hT 2 0, gru z 2 1, front hidT 7, gru agg 3 0, front mlpT 2",
    "gru hT 2 1, front mlp2 3, gru hn 3 0, front mlpT 3, gru agg 3 1, gru r 3 0, gru in 3 0",
    "gru z 3 0, gru hn 3 1, gru r 3 1, gru in 3 1, gru hT 3 0, gru z 3 1, gru agg 4 0",
    "front turn1 0, gru hT 3 1, gru hn 4 0, front turn1 1, front gather 1 0, gru agg 4 1",
    "front gather 1 1, front conv 1 0, front conv 1 1, front convT 1 0, front convT 1 1",
    "gru r 4 0, gru in 4 0, gru z 4 0, gru hn 4 1, gru r 4 1, gru in 4 1, gru z 4 1",
    "front gather 2 0, gru hT 4 0, gru hT 4 1, front gather 2 1, front conv 2 0",
    "front conv 2 1, front convT 2 0, front convT 2 1, next adj 0 0, next adj 0 1",
    "next adj 1 0, next adj 1 1, next adj 2 0, next adj 2 1, next adj 3 0, next adj 3 1",
    "front h0T 0, front h0T 1",
]

ACT_ORDER = [
    "front adj 4 0, front adj 4 1, gru agg 0 0, gru agg 0 1, front adj 5 0, front adj 5 1",
    "front input 0, gru r 0 0, front adj 6 0, front adj 6 1, gru n 0 0, gru z 0 0",
    "front adj 7 0, gru r 0 1, gru hT 0 0, front adj 7 1, gru n 0 1, gru z 0 1, gru hT 0 1",
    "front gather 0 0, front gather 0 1, gru agg 1 0, gru agg 1 1, front square 0, gru r 1 0",
    "front square 1, gru n 1 0, front sigmoid 0, gru z 1 0, gru r 1 1, front sigmoid 1",
    "front hidT 0, front square 2, front square 3, gru hT 1 0, gru n 1 1, gru z 1 1",
    "front hidT 1, front sigmoid 2, front square 4, front square 5, front sigmoid 3",
    "front hidT 2, gru hT 1 1, front mlp2 0, front hidT 3, gru agg 2 0, front square 6",
    "front sigmoid 4, front sigmoid 5, gru agg 2 1, front square 7, gru r 2 0, front hidT 4",
    "front mlp2 1, front hidT 5, front sigmoid 6, gru n 2 0, gru z 2 0, gru r 2 1",
    "front sigmoid 7, front mlp2 2, front hidT 6, gru hT 2 0, front hidT 7, gru n 2 1",
    "gru z 2 1, gru hT 2 1, front mlp2 3, gru agg 3 0, gru agg 3 1, gru r 3 0, front relu1",
    "gru n 3 0, gru z 3 0, gru r 3 1, gru hT 3 0, gru n 3 1, gru z 3 1, front input 1",
    "front turn1 0, gru hT 3 1, front turn1 1, gru agg 4 0, gru agg 4 1, front gather 1 0",
    "front gather 1 1, front conv 1 0, front conv 1 1, gru r 4 0, gru n 4 0, gru z 4 0",
    "front input 2, gru r 4 1, gru n 4 1, gru z 4 1, front gather 2 0, front gather 2 1",
    "front conv 2 0, front conv 2 1, next adj 0 0, next adj 0 1, next adj 1 0, next adj 1 1",
    "next adj 2 0, next adj 2 1, front h0relu 0, front h0relu 1, next adj 3 0, next adj 3 1",
    "front h0n 0, front h0n 1, front h0T 0, front h0T 1",
]

DVE_ORDER = [
    "front stats 0, front var 0, front edge 4, front edge 5, front adj 4 0, front adj 4 1",
    "front norm 0, gru agg 0 0, gru agg 0 1, front adj 5 0, front adj 5 1, front edge 6",
    "gru rhn 0 0, front adj 6 0, gru narg 0 0, front edge 7, front adj 6 1, gru diff 0 0",
    "gru zdiff 0 0, gru h 0 0, front adj 7 0, gru rhn 0 1, gru hT 0 0, front input 0",
    "front adj 7 1, gru narg 0 1, front turn0 0, front turn0 1, gru diff 0 1, gru zdiff 0 1",
    "gru h 0 1, front sum 0, front gather 0 0, gru hT 0 1, front sum 1, front gather 0 1",
    "gru agg 1 0, front mlp1 0, gru agg 1 1, front mlp1 1, gru rhn 1 0, front msq 0",
    "gru narg 1 0, front rms 0, front mlp1 2, gru diff 1 0, front rms 1, gru zdiff 1 0",
    "front mlp1 3, gru h 1 0, front hidT 0, gru rhn 1 1, front msq 1, gru narg 1 1",
    "front mlp1 4, gru hT 1 0, front rms 2, gru diff 1 1, front hidT 1, front mlp1 5",
    "gru zdiff 1 1, front rms 3, gru h 1 1, front msq 2, front rms 4, front hidT 2",
    "gru hT 1 1, front rms 5, front mlp1 6, front hidT 3, gru agg 2 0, front mlp1 7",
    "front mlpT 0, front msq 3, gru rhn 2 0, front rms 6, front hidT 4, gru narg 2 0",
    "gru agg 2 1, front rms 7, front hidT 5, gru diff 2 0, front mlpT 1, gru zdiff 2 0",
    "gru h 2 0, gru rhn 2 1, front hidT 6, gru hT 2 0, gru narg 2 1, front hidT 7",
    "gru diff 2 1, gru zdiff 2 1, gru h 2 1, gru hT 2 1, front mlpT 2, front mlpT 3",
    "front stats 1, front var 1, gru agg 3 0, gru agg 3 1, front norm 1, gru rhn 3 0",
    "gru narg 3 0, front stats 2, gru diff 3 0, front var 2, gru zdiff 3 0, gru h 3 0",
    "gru rhn 3 1, front norm 2, gru narg 3 1, gru hT 3 0, front scale, gru diff 3 1",
    "front shift, gru zdiff 3 1, gru h 3 1, front input 1, front turn1 0, gru hT 3 1",
    "front turn1 1, gru agg 4 0, front gather 1 0, gru agg 4 1, front edges, front gather 1 1",
    "front convT 1 0, front convT 1 1, front stats 3, front var 3, gru rhn 4 0, gru narg 4 0",
    "front norm 3, front input 2, gru diff 4 0, gru zdiff 4 0, gru rhn 4 1, gru narg 4 1",
    "gru h 4 0, gru diff 4 1, gru zdiff 4 1, gru h 4 1, gru hT 4 0, gru hT 4 1",
    "front gather 2 0, front gather 2 1, front convT 2 0, front convT 2 1, next edge 0",
    "next adj 0 0, front stats 4, next adj 0 1, front var 4, next edge 1, next adj 1 0",
    "next adj 1 1, front norm 4, next adj 2 0, next adj 2 1, next edge 2, next edge 3",
    "next adj 3 0, next adj 3 1, front h0n 0, front h0n 1",
]

POOL_ORDER = [
    "front power 0, gru split 1 0, gru split 1 1, front rms 0, front silu 0, front silu 1",
    "front rms 1, front silu 2, gru split 2 0, front rms 2, front silu 3, front silu 4",
    "gru split 2 1, front rms 3, front silu 5, front silu 6, front silu 7, gru split 3 0",
    "front power 1, gru split 3 1, front power 2, gru split 4 0, front skip, gru split 4 1",
    "front power 3, front power 4, front split 0 0, front split 0 1",
]


def adj_preln_kernel(nc, t_in, out):
    x, adj, nodemask = t_in["x"], t_in["adj"], t_in["nodemask"]
    B, N, D = x.shape
    H = t_in["W1"].shape[1]
    L = t_in["WlT"].shape[0]
    KT = N // P
    HB = H // P
    CH = 512
    NC = N // CH
    TC = CH // P
    G3 = 3 * D
    assert D == P and NC == 2 and L == 5 and HB == 4 and KT == 8

    ctx = ExitStack()
    with ctx:
        def sb(name, shape, dt):
            return ctx.enter_context(nc.sbuf_tensor(name, shape, dt))

        def pb(name):
            return ctx.enter_context(nc.psum_tensor(name, [P, CH], F32))

        per = {}

        def sem(name, per_graph):
            s = ctx.enter_context(nc.semaphore(name))
            per[s.name] = per_graph
            return s

        def nth(signal, g, k):
            value = g * per[signal.name] + k
            return max(value, 0) if isinstance(value, int) else value

        def held(eng, value):
            return value if isinstance(value, int) else eng.to_reg(value)

        adjT_hi = sb("adjT_hi", [P, KT, N], F32R)
        adjT_lo = sb("adjT_lo", [P, KT, N], F32R)
        edges_next = sb("edges_next", [P, KT, N], F8)
        edges = sb("edges", [P, KT, N], F8)
        adj_rows = sb("adj_rows", [P, 2, N], F32)
        xf = sb("xf", [P, KT, D], F32)
        xg = sb("xg", [P, KT, D], F32)
        fn_hi = sb("fn_hi", [P, KT, D], F32R)
        fn_lo = sb("fn_lo", [P, KT, D], F32R)
        gn_hi = sb("gn_hi", [P, KT, D], F16)
        gn_lo = sb("gn_lo", [P, KT, D], F16)
        h = sb("h", [P, N], F32)
        h_hi = sb("h_hi", [P, N], F32R)
        h_lo = sb("h_lo", [P, N], F32R)
        s_hi = sb("s_hi", [P, N], F32R)
        s_lo = sb("s_lo", [P, N], F32R)
        r_t = sb("r_t", [P, NC, CH], F32)
        z_t = sb("z_t", [P, NC, CH], F32)
        n_t = sb("n_t", [P, NC, CH], F32)
        ag_hi = sb("ag_hi", [P, N], F32R)
        ag_lo = sb("ag_lo", [P, N], F32R)
        y_hi = sb("y_hi", [P, N], F32R)
        y_lo = sb("y_lo", [P, N], F32R)
        ew = sb("ew", [P, 3 * N], F32)
        mlp_outT = sb("mlp_outT", [P, 2 * P], F32)
        junk = sb("junk", [P, H], BF16)

        NB = H + HB * D + 3 * D + G3
        w_hi = sb("w_hi", [P, NB + L * G3], F32R)
        w_lo = sb("w_lo", [P, NB + L * G3], F32R)
        b1_b = sb("b1_b", [P, H], F32)
        rms_b = sb("rms_b", [P, H], F32)
        gamma_b = sb("gamma_b", [P, D], F32)
        beta_b = sb("beta_b", [P, D], F32)
        ident = sb("ident", [P, P], F32)
        cols = sb("cols", [P, 16], F32)
        mask = sb("mask", [P, KT], F32)
        stats = sb("stats", [P, KT, 6], F32)
        meanvar = sb("meanvar", [P, KT, 2], F32)
        vareps = sb("vareps", [P, KT], F32)
        rstd = sb("rstd", [P, KT], F32)
        ssq = sb("ssq", [P, KT], F32)
        mseps = sb("mseps", [P, KT], F32)
        rrms = sb("rrms", [P, KT], F32)
        neghalf = sb("neghalf", [P, KT], F32)

        c1 = ew[:, 0:N].rearrange("p (t d) -> p t d", d=D)
        c2 = ew[:, N:2 * N].rearrange("p (t d) -> p t d", d=D)
        conv_outT = ew[:, 0:N]
        hid = ew[:, 0:4 * H].rearrange("p (b n) -> p b n", b=4)
        sig = ew[:, 4 * H:6 * H].rearrange("p (b n) -> p b n", b=2)
        ehT = ew[:, N:2 * N]

        raw = ew
        R_IH, R_L = NB, NB + G3
        O_W1, O_W2, O_REL = 0, H, H + HB * D
        O_ROOT, O_L2 = O_REL + D, O_REL + 2 * D
        O_HH, O_G = O_REL + 3 * D, NB

        def w(o, n=P):
            return w_hi[:, o:o + n], w_lo[:, o:o + n]

        B2, BREL, BL2, BIR, BIZ, BIN, BHR, BHZ, BHN, EPSC, BR, BZ = range(12)

        def col(k):
            return cols[:, k:k + 1]

        bank = [pb(f"bank{i}") for i in range(8)]
        P_R, P_Z, P_HN, P_IN = bank[0], bank[1], bank[2], bank[3]
        P_S = bank[4:6]
        P_T = bank[0:2]
        P_F = bank[6:8]

        w_loaded = sem("w_loaded", 0)
        ident_done = sem("ident_done", 0)
        w_hi_done = sem("w_hi_done", 0)
        w_lo_done = sem("w_lo_done", 0)
        fold_done = sem("fold_done", 0)
        bias_done = sem("bias_done", 0)
        setup_done = sem("setup_done", 0)

        adj_in = [sem(f"adj_in{i}", 16 * KT // 2) for i in range(2)]
        x_in = sem("x_in", 16)
        mask_in = sem("mask_in", 16)
        out_stored = sem("out_stored", 32)
        adj_turned = sem("adj_turned", 2 * KT)
        adj_hi_done = sem("adj_hi_done", 2 * KT)
        adj_lo_done = sem("adj_lo_done", 2 * KT)
        edges_done = sem("edges_done", KT)
        edges_taken = sem("edges_taken", 1)

        bn_done = sem("bn_done", 5)
        meanvar_done = sem("meanvar_done", 5)
        vareps_done = sem("vareps_done", 5)
        rstd_done = sem("rstd_done", 5)
        normed = sem("normed", 5)
        scaled = sem("scaled", 1)
        affine = sem("affine", 1)
        relud = sem("relud", 1)
        skip_added = sem("skip_added", 1)
        fn_hi_done = sem("fn_hi_done", 3)
        fn_lo_done = sem("fn_lo_done", 3)
        fn_turned = sem("fn_turned", 4)
        ehT_done = sem("ehT_done", 2)
        hT_hi_done = sem("hT_hi_done", 2)
        hT_lo_done = sem("hT_lo_done", 2)
        ag_done = sem("ag_done", 6)
        ag_summed = sem("ag_summed", 2)
        ag_hi_done = sem("ag_hi_done", 6)
        ag_lo_done = sem("ag_lo_done", 6)
        hid_done = sem("hid_done", KT)
        hid_biased = sem("hid_biased", KT)
        squared = sem("squared", KT)
        mseps_done = sem("mseps_done", KT // 2)
        rrms_done = sem("rrms_done", KT // 2)
        hid_normed = sem("hid_normed", KT)
        sig_done = sem("sig_done", KT)
        silu_done = sem("silu_done", KT)
        hid_turned = sem("hid_turned", KT)
        hidT_hi_done = sem("hidT_hi_done", KT)
        hidT_lo_done = sem("hidT_lo_done", KT)
        mlp_done = sem("mlp_done", KT // 2)
        mlp_biased = sem("mlp_biased", KT // 2)
        mlp_turned = sem("mlp_turned", KT // 2)
        x1_done = sem("x1_done", KT // 2)
        conv_done = sem("conv_done", 4)
        conv_biased = sem("conv_biased", 4)
        conv_turned = sem("conv_turned", 4)
        x2_done = sem("x2_done", 2)
        x3_done = sem("x3_done", 2)
        hr_done = sem("hr_done", 2)
        h0_turned = sem("h0_turned", 2)

        gn_hi_done = sem("gn_hi_done", 2 * L)
        gn_lo_done = sem("gn_lo_done", 2 * L)
        h_new = sem("h_new", 2 * L + 2)
        h_hi_done = sem("h_hi_done", 2 * L)
        h_lo_done = sem("h_lo_done", 2 * L)
        s_done = sem("s_done", 2 * L)
        s_hi_done = sem("s_hi_done", 2 * L)
        s_lo_done = sem("s_lo_done", 2 * L)
        gate_done = sem("gate_done", 8 * L)
        rz_done = sem("rz_done", 4 * L)
        rhn_done = sem("rhn_done", 2 * L)
        narg_done = sem("narg_done", 2 * L)
        n_done = sem("n_done", 2 * L)
        diff_done = sem("diff_done", 2 * L)
        zdiff_done = sem("zdiff_done", 2 * L)
        h_turned = sem("h_turned", 2 * L)
        out_done = sem("out_done", 2)

        block = ctx.enter_context(nc.Block())

        def run(eng, order, stages):
            steps = [step.split() for line in order for step in line.split(", ")]

            def go(g, parts):
                for part, name, *k in steps:
                    if part in parts:
                        stages[name](g + AHEAD[part], *map(int, k))

            go(-2, ("next",))
            go(-1, ("front", "next"))
            go(0, ("gru", "front", "next"))
            with eng.Fori(1, B - 2) as g:
                go(g, ("gru", "front", "next"))
            go(B - 2, ("gru", "front"))
            go(B - 1, ("gru",))

        @block.sync
        def _(sp):
            def load_w(dst, src):
                sp.dma_start(dst, src).then_inc(w_loaded, 16)

            load_w(raw[:, O_W1:O_W1 + H], t_in["W1"])
            load_w(raw[:, O_W2:O_W2 + HB * D].rearrange("p (b d) -> p b d", b=HB),
                   t_in["W2"].rearrange("(b p) d -> p b d", p=P))
            load_w(raw[:, O_REL:O_REL + D], t_in["W_rel"])
            load_w(raw[:, O_ROOT:O_ROOT + D], t_in["W_root"])
            load_w(raw[:, O_L2:O_L2 + D], t_in["W_l2"])
            load_w(raw[:, O_HH:O_HH + G3], t_in["whhT"])
            load_w(raw[:, R_IH:R_IH + G3], t_in["wihT"])
            load_w(raw[:, R_L:R_L + L * D].rearrange("p (l d) -> p l d", l=L),
                   t_in["WlT"].rearrange("l e d -> e l d"))
            for dst, name in ((b1_b, "b1"), (rms_b, "rms"), (gamma_b, "gamma"), (beta_b, "beta")):
                load_w(dst[:, :], t_in[name].partition_broadcast(P))
            load_w(col(EPSC), t_in["epsilon"].partition_broadcast(P))
            for k, name in ((B2, "b2"), (BREL, "b_rel"), (BL2, "b_l2")):
                load_w(col(k), t_in[name].rearrange("(p a) -> p a", a=1))
            load_w(cols[:, BIR:BIR + 3], t_in["b_ih"])
            load_w(cols[:, BHR:BHR + 3], t_in["b_hh"])

            def load_x(f):
                count = held(sp, nth(x3_done, f, 0))
                sp.wait_ge(setup_done, 1)
                sp.wait_ge(x3_done, count)
                sp.dma_start(xf[:, :, :], x[f, :, :].rearrange("(t p) d -> p t d", p=P)
                             ).then_inc(x_in, 16)

            def load_adj(f, t):
                count = held(sp, nth(adj_turned, f, 2 * t - 2))
                sp.wait_ge(setup_done, 1)
                sp.wait_ge(adj_turned, count)
                count = held(sp, nth(edges_done, f, t - 1))
                sp.wait_ge(setup_done, 1)
                sp.wait_ge(edges_done, count)
                sp.dma_start(adj_rows[:, t % 2, :], adj[f, t * P:(t + 1) * P, :]
                             ).then_inc(adj_in[t % 2], 16)

            def load_mask(g):
                count = held(sp, nth(out_done, g, 0))
                sp.wait_ge(setup_done, 1)
                sp.wait_ge(out_done, count)
                sp.dma_start(mask[:, :], nodemask[g, :, :]).then_inc(mask_in, 16)

            def store(g, c):
                count = held(sp, nth(out_done, g, c + 1))
                sp.wait_ge(setup_done, 1)
                sp.wait_ge(out_done, count)
                sp.dma_start(out[g, c * CH:(c + 1) * CH, :].rearrange("(t p) d -> p t d", p=P),
                             xg[:, c * TC:(c + 1) * TC, :]).then_inc(out_stored, 16)

            run(sp, SP_ORDER, {"x": load_x, "adj": load_adj, "mask": load_mask, "store": store})
            sp.wait_ge(out_stored, nth(out_stored, B, 0))

        N_WLOADS = 16 * 18

        @block.tensor
        def _(pe):
            def product(ps, weight, moving, start, stop):
                (wh, wl), (mh, ml) = weight, moving
                pe.matmul(ps, wh, mh, start=start, stop=False)
                pe.matmul(ps, wl, mh, start=False, stop=False)
                return pe.matmul(ps, wh, ml, start=False, stop=stop)

            def turn(ps, tiles):
                for j, tile in enumerate(tiles):
                    last = pe.transpose(ps[:, j * P:(j + 1) * P], tile, ident[:, :])
                return last

            def adj_turn(f, t, q):
                pe.wait_ge(adj_in[t % 2], nth(adj_in[t % 2], f, 16 * (t // 2 + 1)))
                if t == 0:
                    pe.wait_ge(x3_done, nth(x3_done, f, q + 1 - 2))
                if t == HEAD_ADJ:
                    pe.wait_ge(h_new, nth(h_new, f, q + 1 - 12))
                pe.wait_ge(adj_lo_done, nth(adj_lo_done, f, 2 * t + q - 1))
                turn(P_F[q], [adj_rows[:, t % 2, (4 * q + j) * P:(4 * q + j + 1) * P]
                              for j in range(4)]).then_inc(adj_turned, 1)

            def h_turn0(f, c):
                pe.wait_ge(normed, nth(normed, f, 1))
                pe.wait_ge(adj_lo_done, nth(adj_lo_done, f, 2 * (KT - 1) + c + 1))
                turn(P_F[c], [c1[:, c * TC + j, :] for j in range(TC)]).then_inc(fn_turned, 1)

            def gather(f, layer, c):
                pe.wait_ge(fn_lo_done, nth(fn_lo_done, f, layer + 1))
                if layer == 0:
                    pe.wait_ge(adj_lo_done, nth(adj_lo_done, f, 2 * KT))
                    pe.wait_ge(ehT_done, nth(ehT_done, f, c + 1))
                if layer == 1:
                    pe.wait_ge(hT_lo_done, nth(hT_lo_done, f, c + 1))
                if layer == 2:
                    pe.wait_ge(x2_done, nth(x2_done, f, c + 1))
                cs = slice(c * CH, (c + 1) * CH)
                for m in range(KT):
                    last = product(P_F[c][:, :], (fn_hi[:, m, :], fn_lo[:, m, :]),
                                   (adjT_hi[:, m, cs], adjT_lo[:, m, cs]),
                                   start=(m == 0), stop=(m == KT - 1))
                last.then_inc(ag_done, 1)

            def mlp1(f, t):
                if t == 0:
                    pe.wait_ge(ag_lo_done, nth(ag_lo_done, f, 2))
                if t == 6:
                    pe.wait_ge(mlp_biased, nth(mlp_biased, f, 1))
                pe.wait_ge(hid_biased, nth(hid_biased, f, t))
                ns = slice(t * P, (t + 1) * P)
                product(P_F[0][:, :], (ag_hi[:, ns], ag_lo[:, ns]), w(O_W1, H), True, True
                        ).then_inc(hid_done, 1)

            def hid_turn(f, t):
                pe.wait_ge(x1_done, nth(x1_done, f, t // 2 - 1))
                pe.wait_ge(silu_done, nth(silu_done, f, t + 1))
                pe.wait_ge(hidT_lo_done, nth(hidT_lo_done, f, t))
                turn(P_F[1], [hid[:, t % 4, b * P:(b + 1) * P] for b in range(HB)]
                     ).then_inc(hid_turned, 1)

            def mlp2(f, v):
                pe.wait_ge(hidT_lo_done, nth(hidT_lo_done, f, 2 * v + 2))
                pe.wait_ge(hid_biased, nth(hid_biased, f, min(2 * v + 6, KT)))
                pe.wait_ge(mlp_biased, nth(mlp_biased, f, v))
                for b in range(HB):
                    last = product(P_F[0][:, 0:2 * P], w(O_W2 + b * D),
                                   (y_hi[:, b * 2 * P:(b + 1) * 2 * P],
                                    y_lo[:, b * 2 * P:(b + 1) * 2 * P]),
                                   start=(b == 0), stop=(b == HB - 1))
                last.then_inc(mlp_done, 1)

            def mlp_turn(f, v):
                pe.wait_ge(mlp_biased, nth(mlp_biased, f, v + 1))
                pe.wait_ge(hidT_lo_done, nth(hidT_lo_done, f, min(2 * v + 4, KT)))
                pe.wait_ge(x1_done, nth(x1_done, f, v))
                turn(P_F[1], [mlp_outT[:, j * P:(j + 1) * P] for j in range(2)]).then_inc(mlp_turned, 1)

            def h_turn1(f, c):
                pe.wait_ge(affine, nth(affine, f, 1))
                pe.wait_ge(x1_done, nth(x1_done, f, 4))
                turn(P_F[c], [c2[:, c * TC + j, :] for j in range(TC)]).then_inc(fn_turned, 1)

            def conv(f, layer, c):
                cs = slice(c * CH, (c + 1) * CH)
                pe.wait_ge(ag_lo_done, nth(ag_lo_done, f, 2 * layer + 1 + c))
                agg = (ag_hi[:, cs], ag_lo[:, cs])
                if layer == 1:
                    product(P_F[c][:, :], w(O_REL), agg, True, False)
                    last = product(P_F[c][:, :], w(O_ROOT), (y_hi[:, cs], y_lo[:, cs]), False, True)
                else:
                    last = product(P_F[c][:, :], w(O_L2), agg, True, True)
                last.then_inc(conv_done, 1)

            def conv_turn(f, layer, c):
                pe.wait_ge(conv_biased, nth(conv_biased, f, 2 * layer - 2 + c + 1))
                turn(P_F[c], [conv_outT[:, (c * TC + j) * P:(c * TC + j + 1) * P]
                              for j in range(TC)]).then_inc(conv_turned, 1)

            def h0_turn(f, c):
                pe.wait_ge(hr_done, nth(hr_done, f, c + 1))
                if isinstance(f, int) and f == B - 1:
                    pe.wait_ge(x3_done, nth(x3_done, f, c + 1))
                else:
                    pe.wait_ge(adj_lo_done, nth(adj_lo_done, f + 1, 2 * HEAD_ADJ - 1 + c))
                turn(P_F[c], [c1[:, c * TC + j, :] for j in range(TC)]).then_inc(h0_turned, 1)

            def gru_gather(g, s, half):
                if s == 0 and half == 0:
                    count = held(pe, nth(edges_taken, g, 1))
                    pe.wait_ge(setup_done, 1)
                    pe.wait_ge(edges_taken, count)
                count = held(pe, nth(gn_lo_done, g, 2 * s + half + 1))
                pe.wait_ge(setup_done, 1)
                pe.wait_ge(gn_lo_done, count)
                for c in range(NC):
                    for m in range(half * TC, (half + 1) * TC):
                        for part in (gn_hi, gn_lo):
                            last = pe.matmul(P_S[c][:, :], part[:, m, :],
                                             edges[:, m, c * CH:(c + 1) * CH],
                                             start=(m == 0 and part is gn_hi),
                                             stop=(m == KT - 1 and part is gn_lo))
                    if half == 1:
                        last.then_inc(s_done, 1)

            def state(c):
                cs = slice(c * CH, (c + 1) * CH)
                return h_hi[:, cs], h_lo[:, cs]

            def arrived(c):
                cs = slice(c * CH, (c + 1) * CH)
                return s_hi[:, cs], s_lo[:, cs]

            def gate_hn(g, s, c):
                i = 2 * s + c
                pe.wait_ge(h_lo_done, nth(h_lo_done, g, i + 1))
                pe.wait_ge(rhn_done, nth(rhn_done, g, i))
                product(P_HN[:, :], w(O_HH + 2 * D), state(c), True, True).then_inc(gate_done, 1)

            def gate_r(g, s, c):
                i = 2 * s + c
                if i == 0:
                    pe.wait_ge(out_done, nth(out_done, g, 0))
                pe.wait_ge(rz_done, nth(rz_done, g, 2 * i - 1))
                product(P_R[:, :], w(O_HH), state(c), True, False)
                pe.wait_ge(s_lo_done, nth(s_lo_done, g, i + 1))
                product(P_R[:, :], w(O_G + s * G3), arrived(c), False, True).then_inc(gate_done, 1)

            def gate_in(g, s, c):
                i = 2 * s + c
                pe.wait_ge(narg_done, nth(narg_done, g, i))
                product(P_IN[:, :], w(O_G + s * G3 + 2 * D), arrived(c), True, True
                        ).then_inc(gate_done, 1)

            def gate_z(g, s, c):
                i = 2 * s + c
                pe.wait_ge(rz_done, nth(rz_done, g, 2 * i))
                product(P_Z[:, :], w(O_HH + D), state(c), True, False)
                product(P_Z[:, :], w(O_G + s * G3 + D), arrived(c), False, True
                        ).then_inc(gate_done, 1)

            def state_turn(g, s, c):
                pe.wait_ge(h_new, nth(h_new, g, 2 + 2 * s + c + 1))
                pe.wait_ge(rz_done, nth(rz_done, g, 2 * (2 * s + 1) + 1 + c))
                turn(P_T[c], [h[:, (c * TC + j) * P:(c * TC + j + 1) * P] for j in range(TC)]
                     ).then_inc(h_turned, 1)

            pe.wait_ge(w_loaded, N_WLOADS)
            pe.wait_ge(ident_done, 3)
            for l in range(L):
                pe.matmul(bank[l][:, 0:G3], raw[:, R_L + l * D:R_L + (l + 1) * D],
                          raw[:, R_IH:R_IH + G3], start=True, stop=True).then_inc(fold_done, 1)
            pe.wait_ge(w_lo_done, L + 1)
            run(pe, PE_ORDER, {
                "adj": adj_turn, "turn0": h_turn0, "gather": gather, "mlp1": mlp1,
                "hidT": hid_turn, "mlp2": mlp2, "mlpT": mlp_turn, "turn1": h_turn1, "conv": conv,
                "convT": conv_turn, "h0T": h0_turn, "agg": gru_gather, "hn": gate_hn, "r": gate_r,
                "in": gate_in, "z": gate_z, "hT": state_turn})

        @block.scalar
        def _(act):
            def adj_hi(f, t, q):
                act.wait_ge(adj_turned, nth(adj_turned, f, 2 * t + q + 1))
                act.activation(adjT_hi[:, 4 * q:4 * q + 4, t * P:(t + 1) * P],
                               P_F[q][:, :].rearrange("p (j n) -> p j n", j=4), ACT.Copy
                               ).then_inc(adj_hi_done, 1)

            def input_hi(f, layer):
                if layer == 1:
                    act.wait_ge(affine, nth(affine, f, 1))
                    act.activation(fn_hi[:, :, :], c2, ACT.Copy).then_inc(fn_hi_done, 1)
                else:
                    act.wait_ge(normed, nth(normed, f, 1 if layer == 0 else 4))
                    act.activation(fn_hi[:, :, :], c1, ACT.Relu).then_inc(fn_hi_done, 1)

            def agg_hi(f, layer, c):
                cs = slice(c * CH, (c + 1) * CH)
                if layer == 0:
                    act.wait_ge(ag_summed, nth(ag_summed, f, c + 1))
                    act.activation(ag_hi[:, cs], ehT[:, cs], ACT.Copy).then_inc(ag_hi_done, 1)
                else:
                    act.wait_ge(ag_done, nth(ag_done, f, 2 * layer + c + 1))
                    act.activation(ag_hi[:, cs], P_F[c][:, :], ACT.Copy).then_inc(ag_hi_done, 1)

            def square(f, t):
                act.wait_ge(hid_biased, nth(hid_biased, f, t + 1))
                act.wait_ge(squared, nth(squared, f, t))
                act.activation(junk[:, :], hid[:, t % 4, :], ACT.Square,
                               accum_out=ssq[:, t:t + 1]).then_inc(squared, 1)

            def sigmoid(f, t):
                act.wait_ge(hid_normed, nth(hid_normed, f, t + 1))
                act.wait_ge(silu_done, nth(silu_done, f, t - 1))
                act.activation(sig[:, t % 2, :], hid[:, t % 4, :], ACT.Sigmoid).then_inc(sig_done, 1)

            def hidT_hi(f, t):
                act.wait_ge(hid_turned, nth(hid_turned, f, t + 1))
                act.activation(
                    y_hi[:, :].rearrange("p (b n) -> p b n", b=HB)[:, :, (t % 2) * P:(t % 2 + 1) * P],
                    P_F[1][:, :].rearrange("p (b n) -> p b n", b=HB), ACT.Copy
                ).then_inc(hidT_hi_done, 1)

            def mlp_bias(f, v):
                act.wait_ge(mlp_done, nth(mlp_done, f, v + 1))
                act.wait_ge(mlp_turned, nth(mlp_turned, f, v))
                act.activation(mlp_outT[:, :], P_F[0][:, 0:2 * P], ACT.Identity, bias=col(B2)
                               ).then_inc(mlp_biased, 1)

            def relu1(f):
                act.wait_ge(normed, nth(normed, f, 2))
                act.activation(c1, c1, ACT.Relu).then_inc(relud, 1)

            def hT_hi(f, c):
                cs = slice(c * CH, (c + 1) * CH)
                act.wait_ge(fn_turned, nth(fn_turned, f, 2 + c + 1))
                act.activation(y_hi[:, cs], P_F[c][:, :], ACT.Copy).then_inc(hT_hi_done, 1)

            def conv_bias(f, layer, c):
                if layer == 1:
                    act.wait_ge(skip_added, nth(skip_added, f, 1))
                act.wait_ge(conv_done, nth(conv_done, f, 2 * layer - 2 + c + 1))
                act.activation(conv_outT[:, c * CH:(c + 1) * CH], P_F[c][:, :],
                               ACT.Relu if layer == 1 else ACT.Identity,
                               bias=col(BREL if layer == 1 else BL2)).then_inc(conv_biased, 1)

            def h0_relu(f, c):
                part = c1[:, c * TC:(c + 1) * TC, :]
                act.wait_ge(normed, nth(normed, f, 5))
                act.activation(part, part, ACT.Relu, scale=HSCALE).then_inc(hr_done, 1)

            def h0_nodes_hi(f, c):
                ts = slice(c * TC, (c + 1) * TC)
                act.wait_ge(hr_done, nth(hr_done, f, c + 1))
                act.wait_ge(s_done, nth(s_done, f, 0))
                act.activation(gn_hi[:, ts, :], c1[:, ts, :], ACT.Copy).then_inc(gn_hi_done, 1)

            def h0(f, c):
                cs = slice(c * CH, (c + 1) * CH)
                act.wait_ge(h0_turned, nth(h0_turned, f, c + 1))
                act.wait_ge(h_turned, nth(h_turned, f, 0))
                act.activation(h[:, cs], P_F[c][:, :], ACT.Copy, scale=1.0 / HSCALE
                               ).then_inc(h_new, 1)

            def arrived_hi(g, s, c):
                act.wait_ge(s_done, nth(s_done, g, 2 * s + c + 1))
                act.activation(s_hi[:, c * CH:(c + 1) * CH], P_S[c][:, :], ACT.Copy,
                               scale=1.0 / HSCALE).then_inc(s_hi_done, 1)

            def sig_r(g, s, c):
                act.wait_ge(gate_done, nth(gate_done, g, 4 * (2 * s + c) + 2))
                act.activation(r_t[:, c, :], P_R[:, :], ACT.Sigmoid, bias=col(BR)).then_inc(rz_done, 1)

            def sig_z(g, s, c):
                act.wait_ge(gate_done, nth(gate_done, g, 4 * (2 * s + c) + 4))
                act.activation(z_t[:, c, :], P_Z[:, :], ACT.Sigmoid, bias=col(BZ)).then_inc(rz_done, 1)

            def tanh_n(g, s, c):
                act.wait_ge(narg_done, nth(narg_done, g, 2 * s + c + 1))
                act.activation(n_t[:, c, :], n_t[:, c, :], ACT.Tanh, bias=col(BIN)).then_inc(n_done, 1)

            def nodes_hi(g, s, c):
                act.wait_ge(h_turned, nth(h_turned, g, 2 * s + c + 1))
                act.activation(gn_hi[:, c * TC:(c + 1) * TC, :],
                               P_T[c][:, :].rearrange("p (t d) -> p t d", d=D), ACT.Copy,
                               scale=HSCALE).then_inc(gn_hi_done, 1)

            act.wait_ge(w_loaded, N_WLOADS)
            act.activation(w_hi[:, 0:NB], raw[:, 0:NB], ACT.Copy).then_inc(w_hi_done, 1)
            for l in range(L):
                act.wait_ge(fold_done, l + 1)
                act.activation(w_hi[:, O_G + l * G3:O_G + (l + 1) * G3], bank[l][:, 0:G3], ACT.Copy
                               ).then_inc(w_hi_done, 1)
            act.wait_ge(bias_done, 1)
            run(act, ACT_ORDER, {
                "adj": adj_hi, "input": input_hi, "gather": agg_hi, "square": square,
                "sigmoid": sigmoid, "hidT": hidT_hi, "mlp2": mlp_bias, "relu1": relu1,
                "turn1": hT_hi, "conv": conv_bias, "h0relu": h0_relu, "h0n": h0_nodes_hi, "h0T": h0,
                "agg": arrived_hi, "r": sig_r, "z": sig_z, "n": tanh_n, "hT": nodes_hi})

        @block.vector
        def _(dve):
            def norm_in(j):
                return (xf, xf, c1, xf, xg)[j]

            def norm_stats(f, j):
                if j == 0:
                    dve.wait_ge(x_in, nth(x_in, f, 16))
                if j == 1:
                    dve.wait_ge(x1_done, nth(x1_done, f, 4))
                if j == 2:
                    dve.wait_ge(relud, nth(relud, f, 1))
                if j == 3:
                    dve.wait_ge(x2_done, nth(x2_done, f, 2))
                if j == 4:
                    dve.wait_ge(x3_done, nth(x3_done, f, 2))
                for t in range(KT):
                    last = dve.bn_stats(stats[:, t, :], norm_in(j)[:, t, :])
                last.then_inc(bn_done, 1)

            def norm_var(f, j):
                count = held(dve, nth(bn_done, f, j + 1))
                dve.wait_ge(setup_done, 1)
                dve.wait_ge(bn_done, count)
                for t in range(KT):
                    last = dve.bn_aggr(meanvar[:, t, :], stats[:, t, :])
                last.then_inc(meanvar_done, 1)
                dve.wait_ge(meanvar_done, nth(meanvar_done, f, j + 1))
                dve.tensor_scalar(vareps[:, :].unsqueeze(2), meanvar[:, :, 1:2], EPS_LN, None, ALU.add
                                  ).then_inc(vareps_done, 1)

            def norm_apply(f, j):
                dst = c2 if j == 2 else c1
                dve.wait_ge(rstd_done, nth(rstd_done, f, j + 1))
                for t in range(KT):
                    last = dve.tensor_scalar(dst[:, t, :], norm_in(j)[:, t, :], meanvar[:, t, 0:1],
                                             rstd[:, t:t + 1], ALU.subtract, ALU.mult)
                last.then_inc(normed, 1)

            def scale(f):
                dve.wait_ge(normed, nth(normed, f, 3))
                dve.tensor_tensor(c2, c2, gamma_b[:, :].unsqueeze(1).to_broadcast([P, KT, D]), ALU.mult
                                  ).then_inc(scaled, 1)

            def shift(f):
                dve.wait_ge(scaled, nth(scaled, f, 1))
                dve.tensor_tensor(c2, c2, beta_b[:, :].unsqueeze(1).to_broadcast([P, KT, D]), ALU.add
                                  ).then_inc(affine, 1)

            def input_lo(f, layer):
                dve.wait_ge(fn_hi_done, nth(fn_hi_done, f, layer + 1))
                if layer == 1:
                    dve.wait_ge(affine, nth(affine, f, 1))
                    dve.tensor_tensor(fn_lo[:, :, :], c2, fn_hi[:, :, :].bitcast(F32), ALU.subtract
                                      ).then_inc(fn_lo_done, 1)
                else:
                    dve.wait_ge(normed, nth(normed, f, 1 if layer == 0 else 4))
                    dve.scalar_tensor_tensor(fn_lo[:, :, :], c1, 0.0, fn_hi[:, :, :].bitcast(F32),
                                             ALU.max, ALU.subtract).then_inc(fn_lo_done, 1)

            def edge(f, t):
                count = held(dve, nth(adj_in[t % 2], f, 16 * (t // 2 + 1)))
                dve.wait_ge(setup_done, 1)
                dve.wait_ge(adj_in[t % 2], count)
                count = held(dve, nth(edges_taken, f, 0))
                dve.wait_ge(setup_done, 1)
                dve.wait_ge(edges_taken, count)
                dve.tensor_scalar(edges_next[:, t, :], adj_rows[:, t % 2, :], 0.0, None, ALU.not_equal,
                                  saturate=False).then_inc(edges_done, 1)

            def adj_lo(f, t, q):
                js, ns = slice(4 * q, 4 * q + 4), slice(t * P, (t + 1) * P)
                dve.wait_ge(adj_hi_done, nth(adj_hi_done, f, 2 * t + q + 1))
                dve.tensor_tensor(adjT_lo[:, js, ns],
                                  P_F[q][:, :].rearrange("p (j n) -> p j n", j=4),
                                  adjT_hi[:, js, ns].bitcast(F32), ALU.subtract
                                  ).then_inc(adj_lo_done, 1)

            def eps_h(f, c):
                dve.wait_ge(fn_turned, nth(fn_turned, f, c + 1))
                dve.tensor_scalar(ehT[:, c * CH:(c + 1) * CH], P_F[c][:, :], 0.0, col(EPSC),
                                  ALU.max, ALU.mult).then_inc(ehT_done, 1)

            def agg_sum(f, c):
                cs = slice(c * CH, (c + 1) * CH)
                dve.wait_ge(ag_done, nth(ag_done, f, c + 1))
                dve.tensor_tensor(ehT[:, cs], P_F[c][:, :], ehT[:, cs], ALU.add
                                  ).then_inc(ag_summed, 1)

            def agg_lo(f, layer, c):
                cs = slice(c * CH, (c + 1) * CH)
                src = ehT[:, cs] if layer == 0 else P_F[c][:, :]
                dve.wait_ge(ag_hi_done, nth(ag_hi_done, f, 2 * layer + c + 1))
                dve.tensor_tensor(ag_lo[:, cs], src, ag_hi[:, cs].bitcast(F32), ALU.subtract
                                  ).then_inc(ag_lo_done, 1)

            def mlp1_bias(f, t):
                dve.wait_ge(hid_done, nth(hid_done, f, t + 1))
                dve.wait_ge(hid_turned, nth(hid_turned, f, t - 3))
                dve.tensor_tensor(hid[:, t % 4, :], P_F[0][:, :], b1_b[:, :], ALU.add
                                  ).then_inc(hid_biased, 1)

            def mean_square(f, v):
                dve.wait_ge(squared, nth(squared, f, 2 * v + 2))
                dve.tensor_scalar(mseps[:, 2 * v:2 * v + 2], ssq[:, 2 * v:2 * v + 2], 1.0 / H,
                                  EPS_RMS, ALU.mult, ALU.add).then_inc(mseps_done, 1)

            def rms_norm(f, t):
                dve.wait_ge(rrms_done, nth(rrms_done, f, t // 2 + 1))
                dve.scalar_tensor_tensor(hid[:, t % 4, :], hid[:, t % 4, :], rrms[:, t:t + 1],
                                         rms_b[:, :], ALU.mult, ALU.mult).then_inc(hid_normed, 1)

            def hidT_lo(f, t):
                bs = slice((t % 2) * P, (t % 2 + 1) * P)
                dve.wait_ge(hidT_hi_done, nth(hidT_hi_done, f, t + 1))
                dve.tensor_tensor(
                    y_lo[:, :].rearrange("p (b n) -> p b n", b=HB)[:, :, bs],
                    P_F[1][:, :].rearrange("p (b n) -> p b n", b=HB),
                    y_hi[:, :].bitcast(F32).rearrange("p (b n) -> p b n", b=HB)[:, :, bs],
                    ALU.subtract).then_inc(hidT_lo_done, 1)

            def x1(f, v):
                part = xf[:, 2 * v:2 * v + 2, :]
                dve.wait_ge(mlp_turned, nth(mlp_turned, f, v + 1))
                dve.tensor_tensor(part, P_F[1][:, 0:2 * P].rearrange("p (t d) -> p t d", d=D),
                                  part, ALU.add).then_inc(x1_done, 1)

            def hT_lo(f, c):
                cs = slice(c * CH, (c + 1) * CH)
                dve.wait_ge(hT_hi_done, nth(hT_hi_done, f, c + 1))
                dve.tensor_tensor(y_lo[:, cs], P_F[c][:, :], y_hi[:, cs].bitcast(F32), ALU.subtract
                                  ).then_inc(hT_lo_done, 1)

            def conv_add(f, layer, c):
                ts = slice(c * TC, (c + 1) * TC)
                dve.wait_ge(conv_turned, nth(conv_turned, f, 2 * layer - 2 + c + 1))
                src = P_F[c][:, :].rearrange("p (t d) -> p t d", d=D)
                if layer == 1:
                    dve.wait_ge(skip_added, nth(skip_added, f, 1))
                    dve.tensor_tensor(xf[:, ts, :], src, xf[:, ts, :], ALU.add
                                      ).then_inc(x2_done, 1)
                else:
                    dve.wait_ge(out_stored, nth(out_stored, f, 0))
                    dve.tensor_tensor(xg[:, ts, :], src, xf[:, ts, :], ALU.add
                                      ).then_inc(x3_done, 1)

            def take_edges(f):
                dve.wait_ge(s_done, nth(s_done, f, 0))
                dve.wait_ge(edges_done, nth(edges_done, f, KT))
                dve.tensor_copy(edges[:, :, :].bitcast(U16), edges_next[:, :, :].bitcast(U16)
                                ).then_inc(edges_taken, 1)

            def h0_nodes_lo(f, c):
                ts = slice(c * TC, (c + 1) * TC)
                dve.wait_ge(gn_hi_done, nth(gn_hi_done, f, c + 1))
                dve.tensor_tensor(gn_lo[:, ts, :], c1[:, ts, :], gn_hi[:, ts, :], ALU.subtract
                                  ).then_inc(gn_lo_done, 1)

            def arrived_lo(g, s, c):
                cs = slice(c * CH, (c + 1) * CH)
                dve.wait_ge(s_hi_done, nth(s_hi_done, g, 2 * s + c + 1))
                dve.scalar_tensor_tensor(s_lo[:, cs], P_S[c][:, :], 1.0 / HSCALE,
                                         s_hi[:, cs].bitcast(F32), ALU.mult, ALU.subtract
                                         ).then_inc(s_lo_done, 1)

            def r_times_hn(g, s, c):
                i = 2 * s + c
                dve.wait_ge(gate_done, nth(gate_done, g, 4 * i + 1))
                dve.wait_ge(rz_done, nth(rz_done, g, 2 * i + 1))
                dve.scalar_tensor_tensor(n_t[:, c, :], P_HN[:, :], col(BHN), r_t[:, c, :],
                                         ALU.add, ALU.mult).then_inc(rhn_done, 1)

            def n_arg(g, s, c):
                i = 2 * s + c
                dve.wait_ge(gate_done, nth(gate_done, g, 4 * i + 3))
                dve.wait_ge(rhn_done, nth(rhn_done, g, i + 1))
                dve.tensor_tensor(n_t[:, c, :], P_IN[:, :], n_t[:, c, :], ALU.add).then_inc(narg_done, 1)

            def h_minus_n(g, s, c):
                i = 2 * s + c
                cs = slice(c * CH, (c + 1) * CH)
                dve.wait_ge(n_done, nth(n_done, g, i + 1))
                dve.tensor_tensor(r_t[:, c, :], h[:, cs], n_t[:, c, :], ALU.subtract).then_inc(diff_done, 1)

            def times_z(g, s, c):
                i = 2 * s + c
                dve.wait_ge(diff_done, nth(diff_done, g, i + 1))
                dve.wait_ge(rz_done, nth(rz_done, g, 2 * i + 2))
                dve.tensor_tensor(r_t[:, c, :], r_t[:, c, :], z_t[:, c, :], ALU.mult).then_inc(zdiff_done, 1)

            def plus_n(g, s, c):
                i = 2 * s + c
                cs = slice(c * CH, (c + 1) * CH)
                dve.wait_ge(zdiff_done, nth(zdiff_done, g, i + 1))
                dve.tensor_tensor(h[:, cs], r_t[:, c, :], n_t[:, c, :], ALU.add).then_inc(h_new, 1)

            def nodes_lo(g, s, c):
                ts = slice(c * TC, (c + 1) * TC)
                if s < L - 1:
                    dve.wait_ge(gn_hi_done, nth(gn_hi_done, g, 2 * (s + 1) + c + 1))
                    dve.scalar_tensor_tensor(gn_lo[:, ts, :],
                                             P_T[c][:, :].rearrange("p (t d) -> p t d", d=D), HSCALE,
                                             gn_hi[:, ts, :], ALU.mult, ALU.subtract
                                             ).then_inc(gn_lo_done, 1)
                else:
                    dve.wait_ge(h_turned, nth(h_turned, g, 2 * s + c + 1))
                    dve.wait_ge(mask_in, nth(mask_in, g, 16))
                    for j in range(TC):
                        t = c * TC + j
                        last = dve.scalar_tensor_tensor(xg[:, t, :], P_T[c][:, j * P:(j + 1) * P],
                                                        mask[:, t:t + 1], xg[:, t, :],
                                                        ALU.mult, ALU.add)
                    last.then_inc(out_done, 1)

            dve.memset(neghalf[:, :], -0.5).then_inc(ident_done, 1)
            dve.wait_ge(w_loaded, N_WLOADS)
            dve.tensor_tensor(cols[:, BR:BR + 2], cols[:, BIR:BIR + 2], cols[:, BHR:BHR + 2], ALU.add
                              ).then_inc(bias_done, 1)
            dve.memset(ssq[:, :], 0.0).then_inc(setup_done, 1)
            dve.wait_ge(w_hi_done, 1)
            dve.tensor_tensor(w_lo[:, 0:NB], raw[:, 0:NB], w_hi[:, 0:NB].bitcast(F32), ALU.subtract
                              ).then_inc(w_lo_done, 1)
            for l in range(L):
                part = slice(O_G + l * G3, O_G + (l + 1) * G3)
                dve.wait_ge(w_hi_done, l + 2)
                dve.tensor_tensor(w_lo[:, part], bank[l][:, 0:G3], w_hi[:, part].bitcast(F32),
                                  ALU.subtract).then_inc(w_lo_done, 1)
            run(dve, DVE_ORDER, {
                "stats": norm_stats, "var": norm_var, "norm": norm_apply, "scale": scale,
                "shift": shift, "input": input_lo, "edge": edge, "adj": adj_lo, "turn0": eps_h,
                "sum": agg_sum, "gather": agg_lo, "mlp1": mlp1_bias, "msq": mean_square,
                "rms": rms_norm, "hidT": hidT_lo, "mlpT": x1, "turn1": hT_lo, "convT": conv_add,
                "edges": take_edges, "h0n": h0_nodes_lo, "agg": arrived_lo, "rhn": r_times_hn,
                "narg": n_arg, "diff": h_minus_n, "zdiff": times_z, "h": plus_n, "hT": nodes_lo})

        @block.gpsimd
        def _(pool):
            def norm_power(f, j):
                pool.wait_ge(vareps_done, nth(vareps_done, f, j + 1))
                pool.wait_ge(normed, nth(normed, f, j))
                pool.tensor_tensor(rstd[:, :], vareps[:, :], neghalf[:, :], ALU.pow
                                   ).then_inc(rstd_done, 1)

            def add_skip(f):
                pool.wait_ge(relud, nth(relud, f, 1))
                pool.tensor_tensor(xf[:, :, :], xf[:, :, :], c1, ALU.add).then_inc(skip_added, 1)

            def rms_power(f, v):
                pool.wait_ge(mseps_done, nth(mseps_done, f, v + 1))
                pool.tensor_tensor(rrms[:, 2 * v:2 * v + 2], mseps[:, 2 * v:2 * v + 2],
                                   neghalf[:, 0:2], ALU.pow).then_inc(rrms_done, 1)

            def silu(f, t):
                pool.wait_ge(sig_done, nth(sig_done, f, t + 1))
                pool.tensor_tensor(hid[:, t % 4, :], hid[:, t % 4, :], sig[:, t % 2, :],
                                   ALU.mult).then_inc(silu_done, 1)

            def split_state(g, s, c):
                cs = slice(c * CH, (c + 1) * CH)
                count = held(pool, nth(h_new, g, 2 * s + c + 1))
                pool.wait_ge(setup_done, 1)
                pool.wait_ge(h_new, count)
                pool.tensor_scalar(h_hi[:, cs], h[:, cs], 1.0, 0.0, ALU.mult, ALU.add
                                   ).then_inc(h_hi_done, 1)
                pool.wait_ge(h_hi_done, nth(h_hi_done, g, 2 * s + c + 1))
                pool.tensor_tensor(h_lo[:, cs], h[:, cs], h_hi[:, cs].bitcast(F32), ALU.subtract
                                   ).then_inc(h_lo_done, 1)

            pool.memset(ident[:, :], 0.0).then_inc(ident_done, 1)
            pool.wait_ge(ident_done, 2)
            pool.affine_select(out=ident[:, :], in_=ident[:, :], compare_op=ALU.not_equal, fill=1.0,
                               base=0, pattern=[[-1, P]], channel_multiplier=1
                               ).then_inc(ident_done, 1)
            run(pool, POOL_ORDER, {"power": norm_power, "skip": add_skip, "rms": rms_power,
                                   "silu": silu, "split": split_state})


def kernel(**inputs):
    import numpy as _np
    import concourse.bacc as _bacc
    from concourse import mybir as _mybir
    from concourse.bass_utils import run_bass_kernel_spmd as _run

    c = _np.ascontiguousarray
    laid = {
        "x": c(inputs["x"]), "adj": c(inputs["adj"]), "nodemask": c(_np.transpose(inputs["nodemask"].reshape(8, 8, 128), (0, 2, 1))),
        "epsilon": c(inputs["L0_gnn_epsilon"]).reshape(1),
        "W1": c(inputs["L0_gnn_W1"]), "b1": c(inputs["L0_gnn_b1"]), "rms": c(inputs["L0_gnn_rms_weight"]),
        "W2": c(inputs["L0_gnn_W2"]), "b2": c(inputs["L0_gnn_b2"]),
        "W_rel": c(inputs["L1_gnn_W_rel"]), "b_rel": c(inputs["L1_gnn_b_rel"]),
        "W_root": c(inputs["L1_gnn_W_root"]), "gamma": c(inputs["L1_gnn_ln_gamma"]),
        "beta": c(inputs["L1_gnn_ln_beta"]),
        "W_l2": c(inputs["L2_gnn_weight"]), "b_l2": c(inputs["L2_gnn_bias"]),
        "WlT": c(_np.transpose(inputs["L3_gnn_weight"], (0, 2, 1))),
        "wihT": c(_np.transpose(inputs["L3_gnn_w_ih"])), "whhT": c(_np.transpose(inputs["L3_gnn_w_hh"])),
        "b_ih": c(_np.transpose(inputs["L3_gnn_b_ih"].reshape(3, 128))),
        "b_hh": c(_np.transpose(inputs["L3_gnn_b_hh"].reshape(3, 128))),
    }
    nc = _bacc.Bacc("TRN2", target_bir_lowering=False, num_devices=1)
    arrays, args = {}, {}
    for name, a in laid.items():
        arrays[f"in_{name}_dram"] = a
        args[name] = nc.dram_tensor(f"in_{name}_dram", a.shape, _mybir.dt.from_np(a.dtype),
                                    kind="ExternalInput").ap()
    out = nc.dram_tensor("out_0_dram", laid["x"].shape, _mybir.dt.from_np(laid["x"].dtype),
                         kind="ExternalOutput").ap()
    adj_preln_kernel(nc, args, out)
    r = _run(nc, [arrays], core_ids=[0])
    return r.results[0]["out_0_dram"]
```

```python
from contextlib import ExitStack

import concourse.bass as bass
from concourse import mybir

ALU = mybir.AluOpType
ACT = mybir.ActivationFunctionType
F32 = mybir.dt.float32
F32R = mybir.dt.float32r
F16 = mybir.dt.float16
BF16 = mybir.dt.bfloat16
F8 = mybir.dt.float8e4
U16 = mybir.dt.uint16

P = 128
EPS_LN = 1e-5
EPS_RMS = 1e-6
HSCALE = 1024.0


AHEAD = {"gru": 0, "front": 1, "next": 2}
HEAD_ADJ = 4

SP_ORDER = [
    "front adj 4, front adj 5, front adj 6, front adj 7, next adj 0, gru mask, gru store 0",
    "gru store 1, next adj 1, next adj 2, next adj 3, next x",
]

PE_ORDER = [
    "gru agg 0 0 0, front adj 4 0, front adj 4 1, gru agg 0 0 1, front adj 5 0, front adj 5 1",
    "gru agg 0 1 0, gru agg 0 1 1, front adj 6 0, front adj 6 1, gru hn 0 0, gru r 0 0",
    "gru z 0 0, gru in 0 0, front adj 7 0, front adj 7 1, gru hn 0 1, gru r 0 1",
    "front turn0 0, gru z 0 1, front turn0 1, front gather 0 0 0, front gather 0 0 1",
    "gru hT 0 0, gru in 0 1, front gather 0 0 2, front gather 0 0 3, front gather 0 1 0",
    "front gather 0 1 1, front gather 0 1 2, front gather 0 1 3, gru agg 1 0 0, gru agg 1 0 1",
    "front mlp1 0, gru hT 0 1, gru hn 1 0, front mlp1 1, gru agg 1 1 0, gru agg 1 1 1",
    "front mlp1 2, gru r 1 0, front mlp1 3, front hidT 0, gru z 1 0, gru in 1 0, gru hn 1 1",
    "front hidT 1, front mlp1 4, gru r 1 1, front mlp1 5, gru z 1 1, front mlp2 0",
    "front hidT 2, gru hT 1 0, gru in 1 1, front hidT 3, front mlp1 6, gru agg 2 0 0",
    "front mlp1 7, gru agg 2 0 1, gru hT 1 1, front mlpT 0, front mlp2 1, front hidT 4",
    "gru agg 2 1 0, front hidT 5, gru agg 2 1 1, front mlpT 1, front mlp2 2, front hidT 6",
    "gru hn 2 0, gru r 2 0, front hidT 7, gru z 2 0, gru in 2 0, front mlpT 2, front mlp2 3",
    "gru hn 2 1, front mlpT 3, gru r 2 1, gru z 2 1, gru hT 2 0, gru in 2 1, gru agg 3 0 0",
    "gru agg 3 0 1, gru hT 2 1, gru hn 3 0, gru agg 3 1 0, gru agg 3 1 1, gru r 3 0",
    "gru z 3 0, gru in 3 0, front turn1 0, front turn1 1, gru hn 3 1, gru r 3 1, gru z 3 1",
    "front gather 1 0 0, front gather 1 0 1, gru hT 3 0, gru in 3 1, front gather 1 0 2",
    "front gather 1 0 3, gru agg 4 0 0, front gather 1 1 0, gru agg 4 0 1, gru hT 3 1",
    "front gather 1 1 1, front gather 1 1 2, gru agg 4 1 0, gru agg 4 1 1, front gather 1 1 3",
    "front conv 1 0, front conv 1 1, front convT 1 0, front convT 1 1, gru hn 4 0, gru r 4 0",
    "gru z 4 0, gru in 4 0, gru hn 4 1, gru r 4 1, gru z 4 1, gru in 4 1, gru hT 4 0",
    "front gather 2 0 0, front gather 2 0 1, front gather 2 0 2, front gather 2 0 3",
    "gru hT 4 1, front gather 2 1 0, front gather 2 1 1, front gather 2 1 2",
    "front gather 2 1 3, front conv 2 0, front conv 2 1, front convT 2 0, front convT 2 1",
    "next adj 0 0, next adj 0 1, next adj 1 0, next adj 1 1, next adj 2 0, next adj 2 1",
    "next adj 3 0, next adj 3 1, front h0T 0, front h0T 1",
]

ACT_ORDER = [
    "front adj 4 0, front adj 4 1, front adj 5 0, front adj 5 1, gru agg 0 0, front adj 6 0",
    "front adj 6 1, gru agg 0 1, gru r 0 0, front input 0, front adj 7 0, front adj 7 1",
    "gru z 0 0, gru 1-z 0 0, gru n 0 0, gru r 0 1, gru hT 0 0, gru z 0 1, gru 1-z 0 1",
    "gru n 0 1, front gather 0 0, front gather 0 1, gru hT 0 1, front square 0",
    "front square 1, gru agg 1 0, front sigmoid 0, front sigmoid 1, gru agg 1 1",
    "front square 2, gru r 1 0, front hidT 0, front square 3, gru z 1 0, gru 1-z 1 0",
    "front hidT 1, front sigmoid 2, gru n 1 0, front square 4, gru r 1 1, front square 5",
    "front sigmoid 3, front hidT 2, gru hT 1 0, front mlp2 0, gru z 1 1, gru 1-z 1 1",
    "front hidT 3, gru n 1 1, front square 6, front sigmoid 4, front square 7, gru hT 1 1",
    "front sigmoid 5, front mlp2 1, front hidT 4, front sigmoid 6, front hidT 5",
    "front sigmoid 7, gru agg 2 0, front hidT 6, gru agg 2 1, front mlp2 2, gru r 2 0",
    "front hidT 7, gru z 2 0, gru 1-z 2 0, gru n 2 0, front mlp2 3, gru r 2 1, gru hT 2 0",
    "gru z 2 1, gru 1-z 2 1, gru n 2 1, gru hT 2 1, front relu1, gru agg 3 0, gru r 3 0",
    "gru agg 3 1, gru z 3 0, front input 1, gru 1-z 3 0, front turn1 0, gru n 3 0",
    "front turn1 1, gru r 3 1, gru hT 3 0, gru z 3 1, gru 1-z 3 1, gru n 3 1, gru hT 3 1",
    "front gather 1 0, gru agg 4 0, front gather 1 1, front conv 1 0, gru agg 4 1",
    "front conv 1 1, gru r 4 0, gru z 4 0, gru 1-z 4 0, gru n 4 0, gru r 4 1, front input 2",
    "gru z 4 1, gru 1-z 4 1, gru n 4 1, front gather 2 0, front gather 2 1, front conv 2 0",
    "front conv 2 1, next adj 0 0, next adj 0 1, next adj 1 0, next adj 1 1, next adj 2 0",
    "next adj 2 1, front h0relu 0, front h0relu 1, next adj 3 0, next adj 3 1, front h0n 0",
    "front h0n 1, front h0T 0, front h0T 1",
]

DVE_ORDER = [
    "front edge 4, front stats 0, front adj 4 0, front adj 4 1, front var 0, front edge 5",
    "front adj 5 0, front adj 5 1, front norm 0, gru agg 0 0, front adj 6 0, front adj 6 1",
    "gru agg 0 1, front edge 6, gru rhn 0 0, front input 0, front adj 7 0, front adj 7 1",
    "gru narg 0 0, front edge 7, front turn0 0, gru zn 0 0, gru h 0 0, gru rhn 0 1",
    "front turn0 1, gru hT 0 0, gru narg 0 1, gru zn 0 1, gru h 0 1, front sum 0",
    "front gather 0 0, front sum 1, front gather 0 1, front mlp1 0, gru hT 0 1, front mlp1 1",
    "front msq 0, front rms 0, gru agg 1 0, front rms 1, front mlp1 2, gru agg 1 1",
    "front mlp1 3, gru rhn 1 0, front hidT 0, front msq 1, gru narg 1 0, front rms 2",
    "front mlp1 4, front hidT 1, front mlp1 5, gru zn 1 0, front rms 3, front msq 2",
    "gru h 1 0, gru rhn 1 1, front hidT 2, gru hT 1 0, gru narg 1 1, front rms 4",
    "front mlp1 6, gru zn 1 1, front hidT 3, gru h 1 1, front mlp1 7, front rms 5",
    "front mlpT 0, front msq 3, gru hT 1 1, front rms 6, front hidT 4, front hidT 5",
    "front rms 7, front mlpT 1, gru agg 2 0, front hidT 6, gru agg 2 1, gru rhn 2 0",
    "front hidT 7, gru narg 2 0, front mlpT 2, gru zn 2 0, gru h 2 0, front mlpT 3",
    "front stats 1, front var 1, gru rhn 2 1, gru hT 2 0, gru narg 2 1, gru zn 2 1, gru h 2 1",
    "front norm 1, gru hT 2 1, front stats 2, front var 2, gru agg 3 0, front norm 2",
    "front affine, gru rhn 3 0, gru agg 3 1, front input 1, gru narg 3 0, front turn1 0",
    "gru zn 3 0, gru h 3 0, gru rhn 3 1, gru hT 3 0, gru narg 3 1, gru zn 3 1, front turn1 1",
    "gru h 3 1, gru hT 3 1, gru agg 4 0, front gather 1 0, front edges, front gather 1 1",
    "gru agg 4 1, front convT 1 0, front convT 1 1, front stats 3, front var 3, gru rhn 4 0",
    "gru narg 4 0, front norm 3, gru zn 4 0, gru h 4 0, front input 2, gru rhn 4 1",
    "gru narg 4 1, gru hT 4 0, gru zn 4 1, gru h 4 1, front gather 2 0, gru hT 4 1",
    "front gather 2 1, front convT 2 0, front convT 2 1, next edge 0, front stats 4",
    "next adj 0 0, next adj 0 1, next edge 1, front var 4, next adj 1 0, next adj 1 1",
    "next edge 2, front norm 4, next adj 2 0, next adj 2 1, next edge 3, next adj 3 0",
    "next adj 3 1, front h0n 0, front h0n 1",
]

POOL_ORDER = [
    "front power 0, gru zh 0 0, gru zh 0 1, gru split 1 0, front rms 0, gru split 1 1",
    "front silu 0, front silu 1, front rms 1, gru zh 1 0, front silu 2, front rms 2",
    "front silu 3, gru split 2 0, gru zh 1 1, front silu 4, front rms 3, front silu 5",
    "front silu 6, gru split 2 1, front silu 7, gru zh 2 0, gru split 3 0, front power 1",
    "gru zh 2 1, front power 2, gru split 3 1, front skip, gru zh 3 0, gru split 4 0",
    "gru zh 3 1, gru split 4 1, front power 3, gru zh 4 0, gru zh 4 1, front power 4",
    "front split 0 0, front split 0 1",
]


def adj_preln_kernel(nc, t_in, out):
    x, adj, nodemask = t_in["x"], t_in["adj"], t_in["nodemask"]
    B, N, D = x.shape
    H = t_in["W1"].shape[1]
    L = t_in["WlT"].shape[0]
    KT = N // P
    HB = H // P
    CH = 512
    NC = N // CH
    TC = CH // P
    G3 = 3 * D
    assert D == P and NC == 2 and L == 5 and HB == 4 and KT == 8

    ctx = ExitStack()
    with ctx:
        def sb(name, shape, dt):
            return ctx.enter_context(nc.sbuf_tensor(name, shape, dt))

        def pb(name):
            return ctx.enter_context(nc.psum_tensor(name, [P, CH], F32))

        per = {}

        def sem(name, per_graph):
            s = ctx.enter_context(nc.semaphore(name))
            per[s.name] = per_graph
            return s

        def nth(signal, g, k):
            value = g * per[signal.name] + k
            return max(value, 0) if isinstance(value, int) else value

        def held(eng, value):
            return value if isinstance(value, int) else eng.to_reg(value)

        adjT_hi = sb("adjT_hi", [P, KT, N], F32R)
        adjT_lo = sb("adjT_lo", [P, KT, N], F32R)
        edges_next = sb("edges_next", [P, KT, N], F8)
        edges = sb("edges", [P, KT, N], F8)
        adj_rows = sb("adj_rows", [P, 2, N], F32)
        xf = sb("xf", [P, KT, D], F32)
        xg = sb("xg", [P, KT, D], F32)
        fn_hi = sb("fn_hi", [P, KT, D], F32R)
        fn_lo = sb("fn_lo", [P, KT, D], F32R)
        gn_hi = sb("gn_hi", [P, KT, D], F16)
        gn_lo = sb("gn_lo", [P, KT, D], F16)
        h = sb("h", [P, N], F32)
        h_hi = sb("h_hi", [P, N], F32R)
        h_lo = sb("h_lo", [P, N], F32R)
        s_hi = sb("s_hi", [P, N], F32R)
        s_lo = sb("s_lo", [P, N], F32R)
        gru_work = sb("gru_work", [P, 3, NC, CH], F32)
        r_t, z_t = gru_work[:, 0], gru_work[:, 1]
        n_t = gru_work[:, 2]
        ag_hi = sb("ag_hi", [P, N], F32R)
        ag_lo = sb("ag_lo", [P, N], F32R)
        y_hi = sb("y_hi", [P, N], F32R)
        y_lo = sb("y_lo", [P, N], F32R)
        ew = sb("ew", [P, 3 * N], F32)
        mlp_outT = sb("mlp_outT", [P, 2 * P], F32)
        junk = sb("junk", [P, H], BF16)

        NB = H + HB * D + 3 * D + G3
        w_hi = sb("w_hi", [P, NB + L * G3], F32R)
        w_lo = sb("w_lo", [P, NB + L * G3], F32R)
        b1_b = sb("b1_b", [P, H], F32)
        rms_b = sb("rms_b", [P, H], F32)
        gamma_b = sb("gamma_b", [P, D], F32)
        beta_b = sb("beta_b", [P, D], F32)
        ident = sb("ident", [P, P], F32)
        cols = sb("cols", [P, 16], F32)
        mask = sb("mask", [P, KT], F32)
        stats = sb("stats", [P, KT, 6], F32)
        meanvar = sb("meanvar", [P, KT, 2], F32)
        vareps = sb("vareps", [P, KT], F32)
        rstd = sb("rstd", [P, KT], F32)
        ssq = sb("ssq", [P, KT], F32)
        mseps = sb("mseps", [P, KT], F32)
        rrms = sb("rrms", [P, KT], F32)
        neghalf = sb("neghalf", [P, KT], F32)

        c1 = ew[:, 0:N].rearrange("p (t d) -> p t d", d=D)
        c2 = ew[:, N:2 * N].rearrange("p (t d) -> p t d", d=D)
        conv_outT = ew[:, 0:N]
        hid = ew[:, 0:4 * H].rearrange("p (b n) -> p b n", b=4)
        sig = ew[:, 4 * H:6 * H].rearrange("p (b n) -> p b n", b=2)
        ehT = ew[:, N:2 * N]

        raw = gru_work[:, :, :, :].rearrange("p a c n -> p (a c n)")
        R_IH, R_L = NB, NB + G3
        O_W1, O_W2, O_REL = 0, H, H + HB * D
        O_ROOT, O_L2 = O_REL + D, O_REL + 2 * D
        O_HH, O_G = O_REL + 3 * D, NB

        def w(o, n=P):
            return w_hi[:, o:o + n], w_lo[:, o:o + n]

        B2, BREL, BL2, BIR, BIZ, BIN, BHR, BHZ, BHN, EPSC, BR, BZ, NEG_BZ = range(13)

        def col(k):
            return cols[:, k:k + 1]

        bank = [pb(f"bank{i}") for i in range(8)]
        P_R, P_Z, P_HN, P_IN = bank[0], bank[1], bank[2], bank[3]
        P_S = bank[4:6]
        P_T = bank[0:2]
        P_F = bank[6:8]

        w_loaded = sem("w_loaded", 0)
        ident_done = sem("ident_done", 0)
        w_hi_done = sem("w_hi_done", 0)
        w_lo_done = sem("w_lo_done", 0)
        fold_done = sem("fold_done", 0)
        bias_done = sem("bias_done", 0)
        setup_done = sem("setup_done", 0)

        adj_in = [sem(f"adj_in{i}", 16 * KT // 2) for i in range(2)]
        x_in = sem("x_in", 16)
        mask_in = sem("mask_in", 16)
        out_stored = sem("out_stored", 32)
        adj_turned = sem("adj_turned", 2 * KT)
        adj_hi_done = sem("adj_hi_done", 2 * KT)
        adj_lo_done = sem("adj_lo_done", 2 * KT)
        edges_done = sem("edges_done", KT)
        edges_taken = sem("edges_taken", 1)

        bn_done = sem("bn_done", 5)
        meanvar_done = sem("meanvar_done", 5)
        vareps_done = sem("vareps_done", 5)
        rstd_done = sem("rstd_done", 5)
        normed = sem("normed", 5)
        affine = sem("affine", 1)
        relud = sem("relud", 1)
        skip_added = sem("skip_added", 1)
        fn_hi_done = sem("fn_hi_done", 3)
        fn_lo_done = sem("fn_lo_done", 3)
        fn_turned = sem("fn_turned", 4)
        ehT_done = sem("ehT_done", 2)
        hT_hi_done = sem("hT_hi_done", 2)
        hT_lo_done = sem("hT_lo_done", 2)
        ag_done = sem("ag_done", 6)
        ag_summed = sem("ag_summed", 2)
        ag_hi_done = sem("ag_hi_done", 6)
        ag_lo_done = sem("ag_lo_done", 6)
        hid_done = sem("hid_done", KT)
        hid_biased = sem("hid_biased", KT)
        squared = sem("squared", KT)
        mseps_done = sem("mseps_done", KT // 2)
        rrms_done = sem("rrms_done", KT // 2)
        hid_normed = sem("hid_normed", KT)
        sig_done = sem("sig_done", KT)
        silu_done = sem("silu_done", KT)
        hid_turned = sem("hid_turned", KT)
        hidT_hi_done = sem("hidT_hi_done", KT)
        hidT_lo_done = sem("hidT_lo_done", KT)
        mlp_done = sem("mlp_done", KT // 2)
        mlp_biased = sem("mlp_biased", KT // 2)
        mlp_turned = sem("mlp_turned", KT // 2)
        x1_done = sem("x1_done", KT // 2)
        conv_done = sem("conv_done", 4)
        conv_biased = sem("conv_biased", 4)
        conv_turned = sem("conv_turned", 4)
        x2_done = sem("x2_done", 2)
        x3_done = sem("x3_done", 2)
        hr_done = sem("hr_done", 2)
        h0_turned = sem("h0_turned", 2)

        gn_hi_done = sem("gn_hi_done", 2 * L)
        gn_lo_done = sem("gn_lo_done", 2 * L)
        h_new = sem("h_new", 2 * L + 2)
        h_hi_done = sem("h_hi_done", 2 * L)
        h_lo_done = sem("h_lo_done", 2 * L)
        s_done = sem("s_done", 2 * L)
        s_hi_done = sem("s_hi_done", 2 * L)
        s_lo_done = sem("s_lo_done", 2 * L)
        gate_done = sem("gate_done", 8 * L)
        rz_done = sem("rz_done", 4 * L)
        rhn_done = sem("rhn_done", 2 * L)
        narg_done = sem("narg_done", 2 * L)
        n_done = sem("n_done", 2 * L)
        keep_done = sem("keep_done", 2 * L)
        new_part_done = sem("new_part_done", 2 * L)
        old_part_done = sem("old_part_done", 2 * L)
        h_turned = sem("h_turned", 2 * L)
        out_done = sem("out_done", 2)

        block = ctx.enter_context(nc.Block())

        def run(eng, order, stages, prepare=lambda: None):
            steps = [step.split() for line in order for step in line.split(", ")]

            def go(g, parts):
                for part, name, *k in steps:
                    if part in parts:
                        stages[name](g + AHEAD[part], *map(int, k))

            go(-2, ("next",))
            prepare()
            go(-1, ("front", "next"))
            go(0, ("gru", "front", "next"))
            with eng.Fori(1, B - 2) as g:
                go(g, ("gru", "front", "next"))
            go(B - 2, ("gru", "front"))
            go(B - 1, ("gru",))

        @block.sync
        def _(sp):
            def load_x(f):
                count = held(sp, nth(x3_done, f, 0))
                sp.wait_ge(setup_done, 1)
                sp.wait_ge(x3_done, count)
                sp.dma_start(xf[:, :, :], x[f, :, :].rearrange("(t p) d -> p t d", p=P)
                             ).then_inc(x_in, 16)

            def load_adj(f, t):
                count = held(sp, nth(adj_turned, f, 2 * t - 2))
                sp.wait_ge(setup_done, 1)
                sp.wait_ge(adj_turned, count)
                count = held(sp, nth(edges_done, f, t - 1))
                sp.wait_ge(setup_done, 1)
                sp.wait_ge(edges_done, count)
                sp.dma_start(adj_rows[:, t % 2, :], adj[f, t * P:(t + 1) * P, :]
                             ).then_inc(adj_in[t % 2], 16)

            def load_mask(g):
                count = held(sp, nth(out_done, g, 0))
                sp.wait_ge(setup_done, 1)
                sp.wait_ge(out_done, count)
                sp.dma_start(mask[:, :], nodemask[g, :, :]).then_inc(mask_in, 16)

            def store(g, c):
                count = held(sp, nth(out_done, g, c + 1))
                sp.wait_ge(setup_done, 1)
                sp.wait_ge(out_done, count)
                sp.dma_start(out[g, c * CH:(c + 1) * CH, :].rearrange("(t p) d -> p t d", p=P),
                             xg[:, c * TC:(c + 1) * TC, :]).then_inc(out_stored, 16)

            run(sp, SP_ORDER, {"x": load_x, "adj": load_adj, "mask": load_mask, "store": store})
            sp.wait_ge(out_stored, nth(out_stored, B, 0))

        N_WLOADS = 16 * 18

        @block.tensor
        def _(pe):
            def product(ps, weight, moving, start, stop):
                (wh, wl), (mh, ml) = weight, moving
                pe.matmul(ps, wh, mh, start=start, stop=False)
                pe.matmul(ps, wl, mh, start=False, stop=False)
                return pe.matmul(ps, wh, ml, start=False, stop=stop)

            def turn(ps, tiles):
                for j, tile in enumerate(tiles):
                    last = pe.transpose(ps[:, j * P:(j + 1) * P], tile, ident[:, :])
                return last

            def adj_turn(f, t, q):
                pe.wait_ge(adj_in[t % 2], nth(adj_in[t % 2], f, 16 * (t // 2 + 1)))
                if t == 0:
                    pe.wait_ge(x3_done, nth(x3_done, f, q + 1 - 2))
                if t == HEAD_ADJ:
                    pe.wait_ge(h_new, nth(h_new, f, q + 1 - 12))
                pe.wait_ge(adj_lo_done, nth(adj_lo_done, f, 2 * t + q - 1))
                turn(P_F[q], [adj_rows[:, t % 2, (4 * q + j) * P:(4 * q + j + 1) * P]
                              for j in range(4)]).then_inc(adj_turned, 1)

            def h_turn0(f, c):
                pe.wait_ge(normed, nth(normed, f, 1))
                pe.wait_ge(adj_lo_done, nth(adj_lo_done, f, 2 * (KT - 1) + c + 1))
                turn(P_F[c], [c1[:, c * TC + j, :] for j in range(TC)]).then_inc(fn_turned, 1)

            def gather(f, layer, c, quarter):
                pe.wait_ge(fn_lo_done, nth(fn_lo_done, f, layer + 1))
                if layer == 0:
                    pe.wait_ge(adj_lo_done, nth(adj_lo_done, f, 2 * KT))
                    pe.wait_ge(ehT_done, nth(ehT_done, f, c + 1))
                if layer == 1:
                    pe.wait_ge(hT_lo_done, nth(hT_lo_done, f, c + 1))
                if layer == 2:
                    pe.wait_ge(x2_done, nth(x2_done, f, c + 1))
                cs = slice(c * CH, (c + 1) * CH)
                for m in range(quarter * KT // 4, (quarter + 1) * KT // 4):
                    last = product(P_F[c][:, :], (fn_hi[:, m, :], fn_lo[:, m, :]),
                                   (adjT_hi[:, m, cs], adjT_lo[:, m, cs]),
                                   start=(m == 0), stop=(m == KT - 1))
                if quarter == 3:
                    last.then_inc(ag_done, 1)

            def mlp1(f, t):
                if t == 0:
                    pe.wait_ge(w_lo_done, 1)
                    pe.wait_ge(ag_lo_done, nth(ag_lo_done, f, 2))
                if t == 6:
                    pe.wait_ge(mlp_biased, nth(mlp_biased, f, 1))
                pe.wait_ge(hid_biased, nth(hid_biased, f, t))
                ns = slice(t * P, (t + 1) * P)
                product(P_F[0][:, :], (ag_hi[:, ns], ag_lo[:, ns]), w(O_W1, H), True, True
                        ).then_inc(hid_done, 1)

            def hid_turn(f, t):
                pe.wait_ge(x1_done, nth(x1_done, f, t // 2 - 1))
                pe.wait_ge(silu_done, nth(silu_done, f, t + 1))
                pe.wait_ge(hidT_lo_done, nth(hidT_lo_done, f, t))
                turn(P_F[1], [hid[:, t % 4, b * P:(b + 1) * P] for b in range(HB)]
                     ).then_inc(hid_turned, 1)

            def mlp2(f, v):
                pe.wait_ge(hidT_lo_done, nth(hidT_lo_done, f, 2 * v + 2))
                pe.wait_ge(hid_biased, nth(hid_biased, f, min(2 * v + 6, KT)))
                pe.wait_ge(mlp_biased, nth(mlp_biased, f, v))
                for b in range(HB):
                    last = product(P_F[0][:, 0:2 * P], w(O_W2 + b * D),
                                   (y_hi[:, b * 2 * P:(b + 1) * 2 * P],
                                    y_lo[:, b * 2 * P:(b + 1) * 2 * P]),
                                   start=(b == 0), stop=(b == HB - 1))
                last.then_inc(mlp_done, 1)

            def mlp_turn(f, v):
                pe.wait_ge(mlp_biased, nth(mlp_biased, f, v + 1))
                pe.wait_ge(hidT_lo_done, nth(hidT_lo_done, f, min(2 * v + 4, KT)))
                pe.wait_ge(x1_done, nth(x1_done, f, v))
                turn(P_F[1], [mlp_outT[:, j * P:(j + 1) * P] for j in range(2)]).then_inc(mlp_turned, 1)

            def h_turn1(f, c):
                pe.wait_ge(affine, nth(affine, f, 1))
                pe.wait_ge(x1_done, nth(x1_done, f, 4))
                turn(P_F[c], [c2[:, c * TC + j, :] for j in range(TC)]).then_inc(fn_turned, 1)

            def conv(f, layer, c):
                cs = slice(c * CH, (c + 1) * CH)
                pe.wait_ge(ag_lo_done, nth(ag_lo_done, f, 2 * layer + 1 + c))
                agg = (ag_hi[:, cs], ag_lo[:, cs])
                if layer == 1:
                    product(P_F[c][:, :], w(O_REL), agg, True, False)
                    last = product(P_F[c][:, :], w(O_ROOT), (y_hi[:, cs], y_lo[:, cs]), False, True)
                else:
                    last = product(P_F[c][:, :], w(O_L2), agg, True, True)
                last.then_inc(conv_done, 1)

            def conv_turn(f, layer, c):
                pe.wait_ge(conv_biased, nth(conv_biased, f, 2 * layer - 2 + c + 1))
                turn(P_F[c], [conv_outT[:, (c * TC + j) * P:(c * TC + j + 1) * P]
                              for j in range(TC)]).then_inc(conv_turned, 1)

            def h0_turn(f, c):
                pe.wait_ge(hr_done, nth(hr_done, f, c + 1))
                if isinstance(f, int) and f == B - 1:
                    pe.wait_ge(x3_done, nth(x3_done, f, c + 1))
                else:
                    pe.wait_ge(adj_lo_done, nth(adj_lo_done, f + 1, 2 * HEAD_ADJ - 1 + c))
                turn(P_F[c], [c1[:, c * TC + j, :] for j in range(TC)]).then_inc(h0_turned, 1)

            def gru_gather(g, s, half, c):
                if s == 0 and half == 0 and c == 0:
                    count = held(pe, nth(edges_taken, g, 1))
                    pe.wait_ge(setup_done, 1)
                    pe.wait_ge(edges_taken, count)
                count = held(pe, nth(gn_lo_done, g, 2 * s + half + 1))
                pe.wait_ge(setup_done, 1)
                pe.wait_ge(gn_lo_done, count)
                for m in range(half * TC, (half + 1) * TC):
                    for part in (gn_hi, gn_lo):
                        last = pe.matmul(P_S[c][:, :], part[:, m, :],
                                         edges[:, m, c * CH:(c + 1) * CH],
                                         start=(m == 0 and part is gn_hi),
                                         stop=(m == KT - 1 and part is gn_lo))
                if half == 1:
                    last.then_inc(s_done, 1)

            def state(c):
                cs = slice(c * CH, (c + 1) * CH)
                return h_hi[:, cs], h_lo[:, cs]

            def arrived(c):
                cs = slice(c * CH, (c + 1) * CH)
                return s_hi[:, cs], s_lo[:, cs]

            def gate_hn(g, s, c):
                i = 2 * s + c
                pe.wait_ge(h_lo_done, nth(h_lo_done, g, i + 1))
                pe.wait_ge(rhn_done, nth(rhn_done, g, i))
                product(P_HN[:, :], w(O_HH + 2 * D), state(c), True, True).then_inc(gate_done, 1)

            def gate_r(g, s, c):
                i = 2 * s + c
                pe.wait_ge(w_lo_done, L + 1)
                if i == 0:
                    pe.wait_ge(out_done, nth(out_done, g, 0))
                pe.wait_ge(rz_done, nth(rz_done, g, 2 * i - 1))
                product(P_R[:, :], w(O_HH), state(c), True, False)
                pe.wait_ge(s_lo_done, nth(s_lo_done, g, i + 1))
                product(P_R[:, :], w(O_G + s * G3), arrived(c), False, True).then_inc(gate_done, 1)

            def gate_z(g, s, c):
                i = 2 * s + c
                pe.wait_ge(keep_done, nth(keep_done, g, i))
                product(P_Z[:, :], w(O_HH + D), state(c), True, False)
                product(P_Z[:, :], w(O_G + s * G3 + D), arrived(c), False, True
                        ).then_inc(gate_done, 1)

            def gate_in(g, s, c):
                i = 2 * s + c
                pe.wait_ge(narg_done, nth(narg_done, g, i))
                product(P_IN[:, :], w(O_G + s * G3 + 2 * D), arrived(c), True, True
                        ).then_inc(gate_done, 1)

            def state_turn(g, s, c):
                pe.wait_ge(h_new, nth(h_new, g, 2 + 2 * s + c + 1))
                if c == 0:
                    pe.wait_ge(rz_done, nth(rz_done, g, 4 * s + 3))
                else:
                    pe.wait_ge(keep_done, nth(keep_done, g, 2 * s + 2))
                turn(P_T[c], [h[:, (c * TC + j) * P:(c * TC + j + 1) * P] for j in range(TC)]
                     ).then_inc(h_turned, 1)

            def fold_weights():
                pe.wait_ge(w_loaded, N_WLOADS)
                for l in range(L):
                    pe.matmul(bank[l][:, 0:G3], raw[:, R_L + l * D:R_L + (l + 1) * D],
                              raw[:, R_IH:R_IH + G3], start=True, stop=True).then_inc(fold_done, 1)

            pe.wait_ge(ident_done, 3)
            run(pe, PE_ORDER, {
                "adj": adj_turn, "turn0": h_turn0, "gather": gather, "mlp1": mlp1,
                "hidT": hid_turn, "mlp2": mlp2, "mlpT": mlp_turn, "turn1": h_turn1, "conv": conv,
                "convT": conv_turn, "h0T": h0_turn, "agg": gru_gather, "hn": gate_hn, "r": gate_r,
                "in": gate_in, "z": gate_z, "hT": state_turn}, fold_weights)

        @block.scalar
        def _(act):
            def load_w(dst, src):
                act.dma_start(dst, src).then_inc(w_loaded, 16)

            load_w(raw[:, O_W1:O_W1 + H], t_in["W1"])
            load_w(raw[:, O_W2:O_W2 + HB * D].rearrange("p (b d) -> p b d", b=HB),
                   t_in["W2"].rearrange("(b p) d -> p b d", p=P))
            load_w(raw[:, O_REL:O_REL + D], t_in["W_rel"])
            load_w(raw[:, O_ROOT:O_ROOT + D], t_in["W_root"])
            load_w(raw[:, O_L2:O_L2 + D], t_in["W_l2"])
            load_w(raw[:, O_HH:O_HH + G3], t_in["whhT"])
            load_w(raw[:, R_IH:R_IH + G3], t_in["wihT"])
            load_w(raw[:, R_L:R_L + L * D].rearrange("p (l d) -> p l d", l=L),
                   t_in["WlT"].rearrange("l e d -> e l d"))
            for dst, name in ((b1_b, "b1"), (rms_b, "rms"), (gamma_b, "gamma"), (beta_b, "beta")):
                load_w(dst[:, :], t_in[name].partition_broadcast(P))
            load_w(col(EPSC), t_in["epsilon"].partition_broadcast(P))
            for k, name in ((B2, "b2"), (BREL, "b_rel"), (BL2, "b_l2")):
                load_w(col(k), t_in[name].rearrange("(p a) -> p a", a=1))
            load_w(cols[:, BIR:BIR + 3], t_in["b_ih"])
            load_w(cols[:, BHR:BHR + 3], t_in["b_hh"])

            def adj_hi(f, t, q):
                act.wait_ge(adj_turned, nth(adj_turned, f, 2 * t + q + 1))
                act.activation(adjT_hi[:, 4 * q:4 * q + 4, t * P:(t + 1) * P],
                               P_F[q][:, :].rearrange("p (j n) -> p j n", j=4), ACT.Copy
                               ).then_inc(adj_hi_done, 1)

            def input_hi(f, layer):
                if layer == 1:
                    act.wait_ge(affine, nth(affine, f, 1))
                    act.activation(fn_hi[:, :, :], c2, ACT.Copy).then_inc(fn_hi_done, 1)
                else:
                    act.wait_ge(normed, nth(normed, f, 1 if layer == 0 else 4))
                    act.activation(fn_hi[:, :, :], c1, ACT.Relu).then_inc(fn_hi_done, 1)

            def agg_hi(f, layer, c):
                cs = slice(c * CH, (c + 1) * CH)
                if layer == 0:
                    act.wait_ge(ag_summed, nth(ag_summed, f, c + 1))
                    act.activation(ag_hi[:, cs], ehT[:, cs], ACT.Copy).then_inc(ag_hi_done, 1)
                else:
                    act.wait_ge(ag_done, nth(ag_done, f, 2 * layer + c + 1))
                    act.activation(ag_hi[:, cs], P_F[c][:, :], ACT.Copy).then_inc(ag_hi_done, 1)

            def square(f, t):
                act.wait_ge(hid_biased, nth(hid_biased, f, t + 1))
                act.wait_ge(squared, nth(squared, f, t))
                act.activation(junk[:, :], hid[:, t % 4, :], ACT.Square,
                               accum_out=ssq[:, t:t + 1]).then_inc(squared, 1)

            def sigmoid(f, t):
                act.wait_ge(hid_normed, nth(hid_normed, f, t + 1))
                act.wait_ge(silu_done, nth(silu_done, f, t - 1))
                act.activation(sig[:, t % 2, :], hid[:, t % 4, :], ACT.Sigmoid).then_inc(sig_done, 1)

            def hidT_hi(f, t):
                act.wait_ge(hid_turned, nth(hid_turned, f, t + 1))
                act.activation(
                    y_hi[:, :].rearrange("p (b n) -> p b n", b=HB)[:, :, (t % 2) * P:(t % 2 + 1) * P],
                    P_F[1][:, :].rearrange("p (b n) -> p b n", b=HB), ACT.Copy
                ).then_inc(hidT_hi_done, 1)

            def mlp_bias(f, v):
                act.wait_ge(mlp_done, nth(mlp_done, f, v + 1))
                act.wait_ge(mlp_turned, nth(mlp_turned, f, v))
                act.activation(mlp_outT[:, :], P_F[0][:, 0:2 * P], ACT.Identity, bias=col(B2)
                               ).then_inc(mlp_biased, 1)

            def relu1(f):
                act.wait_ge(normed, nth(normed, f, 2))
                act.activation(c1, c1, ACT.Relu).then_inc(relud, 1)

            def hT_hi(f, c):
                cs = slice(c * CH, (c + 1) * CH)
                act.wait_ge(fn_turned, nth(fn_turned, f, 2 + c + 1))
                act.activation(y_hi[:, cs], P_F[c][:, :], ACT.Copy).then_inc(hT_hi_done, 1)

            def conv_bias(f, layer, c):
                if layer == 1:
                    act.wait_ge(skip_added, nth(skip_added, f, 1))
                act.wait_ge(conv_done, nth(conv_done, f, 2 * layer - 2 + c + 1))
                act.activation(conv_outT[:, c * CH:(c + 1) * CH], P_F[c][:, :],
                               ACT.Relu if layer == 1 else ACT.Identity,
                               bias=col(BREL if layer == 1 else BL2)).then_inc(conv_biased, 1)

            def h0_relu(f, c):
                part = c1[:, c * TC:(c + 1) * TC, :]
                act.wait_ge(normed, nth(normed, f, 5))
                act.activation(part, part, ACT.Relu, scale=HSCALE).then_inc(hr_done, 1)

            def h0_nodes_hi(f, c):
                ts = slice(c * TC, (c + 1) * TC)
                act.wait_ge(hr_done, nth(hr_done, f, c + 1))
                act.wait_ge(s_done, nth(s_done, f, 0))
                act.activation(gn_hi[:, ts, :], c1[:, ts, :], ACT.Copy).then_inc(gn_hi_done, 1)

            def h0(f, c):
                cs = slice(c * CH, (c + 1) * CH)
                act.wait_ge(h0_turned, nth(h0_turned, f, c + 1))
                act.wait_ge(h_turned, nth(h_turned, f, 0))
                act.activation(h[:, cs], P_F[c][:, :], ACT.Copy, scale=1.0 / HSCALE
                               ).then_inc(h_new, 1)

            def arrived_hi(g, s, c):
                act.wait_ge(s_done, nth(s_done, g, 2 * s + c + 1))
                act.activation(s_hi[:, c * CH:(c + 1) * CH], P_S[c][:, :], ACT.Copy,
                               scale=1.0 / HSCALE).then_inc(s_hi_done, 1)

            def sig_r(g, s, c):
                act.wait_ge(gate_done, nth(gate_done, g, 4 * (2 * s + c) + 2))
                act.activation(r_t[:, c, :], P_R[:, :], ACT.Sigmoid, bias=col(BR)).then_inc(rz_done, 1)

            def sig_z(g, s, c):
                act.wait_ge(gate_done, nth(gate_done, g, 4 * (2 * s + c) + 3))
                act.activation(z_t[:, c, :], P_Z[:, :], ACT.Sigmoid, bias=col(BZ)).then_inc(rz_done, 1)

            def one_minus_z(g, s, c):
                i = 2 * s + c
                act.wait_ge(gate_done, nth(gate_done, g, 4 * i + 3))
                act.wait_ge(rhn_done, nth(rhn_done, g, i + 1))
                act.activation(r_t[:, c, :], P_Z[:, :], ACT.Sigmoid, bias=col(NEG_BZ), scale=-1.0
                               ).then_inc(keep_done, 1)

            def tanh_n(g, s, c):
                act.wait_ge(narg_done, nth(narg_done, g, 2 * s + c + 1))
                act.activation(n_t[:, c, :], n_t[:, c, :], ACT.Tanh, bias=col(BIN)).then_inc(n_done, 1)

            def nodes_hi(g, s, c):
                act.wait_ge(h_turned, nth(h_turned, g, 2 * s + c + 1))
                act.activation(gn_hi[:, c * TC:(c + 1) * TC, :],
                               P_T[c][:, :].rearrange("p (t d) -> p t d", d=D), ACT.Copy,
                               scale=HSCALE).then_inc(gn_hi_done, 1)

            def split_weights():
                act.wait_ge(w_loaded, N_WLOADS)
                act.activation(w_hi[:, 0:NB], raw[:, 0:NB], ACT.Copy).then_inc(w_hi_done, 1)
                for l in range(L):
                    act.wait_ge(fold_done, l + 1)
                    act.activation(w_hi[:, O_G + l * G3:O_G + (l + 1) * G3], bank[l][:, 0:G3], ACT.Copy
                                   ).then_inc(w_hi_done, 1)
                act.wait_ge(bias_done, 2)

            run(act, ACT_ORDER, {
                "adj": adj_hi, "input": input_hi, "gather": agg_hi, "square": square,
                "sigmoid": sigmoid, "hidT": hidT_hi, "mlp2": mlp_bias, "relu1": relu1,
                "turn1": hT_hi, "conv": conv_bias, "h0relu": h0_relu, "h0n": h0_nodes_hi, "h0T": h0,
                "agg": arrived_hi, "r": sig_r, "z": sig_z, "1-z": one_minus_z, "n": tanh_n, "hT": nodes_hi}, split_weights)

        @block.vector
        def _(dve):
            def norm_in(j):
                return (xf, xf, c1, xf, xg)[j]

            def norm_stats(f, j):
                if j == 0:
                    dve.wait_ge(x_in, nth(x_in, f, 16))
                if j == 1:
                    dve.wait_ge(x1_done, nth(x1_done, f, 4))
                if j == 2:
                    dve.wait_ge(relud, nth(relud, f, 1))
                if j == 3:
                    dve.wait_ge(x2_done, nth(x2_done, f, 2))
                if j == 4:
                    dve.wait_ge(x3_done, nth(x3_done, f, 2))
                for t in range(KT):
                    last = dve.bn_stats(stats[:, t, :], norm_in(j)[:, t, :])
                last.then_inc(bn_done, 1)

            def norm_var(f, j):
                count = held(dve, nth(bn_done, f, j + 1))
                dve.wait_ge(setup_done, 1)
                dve.wait_ge(bn_done, count)
                for t in range(KT):
                    last = dve.bn_aggr(meanvar[:, t, :], stats[:, t, :])
                last.then_inc(meanvar_done, 1)
                dve.wait_ge(meanvar_done, nth(meanvar_done, f, j + 1))
                dve.tensor_scalar(vareps[:, :].unsqueeze(2), meanvar[:, :, 1:2], EPS_LN, None, ALU.add
                                  ).then_inc(vareps_done, 1)

            def norm_apply(f, j):
                if j == 2:
                    for t in range(KT):
                        last = dve.scalar_tensor_tensor(c2[:, t, :], c1[:, t, :], meanvar[:, t, 0:1],
                                                        gamma_b[:, :], ALU.subtract, ALU.mult)
                    last.then_inc(normed, 1)
                    return
                dst = c1
                dve.wait_ge(rstd_done, nth(rstd_done, f, j + 1))
                for t in range(KT):
                    last = dve.tensor_scalar(dst[:, t, :], norm_in(j)[:, t, :], meanvar[:, t, 0:1],
                                             rstd[:, t:t + 1], ALU.subtract, ALU.mult)
                last.then_inc(normed, 1)

            def affine_apply(f):
                dve.wait_ge(rstd_done, nth(rstd_done, f, 3))
                dve.wait_ge(normed, nth(normed, f, 3))
                for t in range(KT):
                    last = dve.scalar_tensor_tensor(c2[:, t, :], c2[:, t, :], rstd[:, t:t + 1],
                                                    beta_b[:, :], ALU.mult, ALU.add)
                last.then_inc(affine, 1)

            def input_lo(f, layer):
                dve.wait_ge(fn_hi_done, nth(fn_hi_done, f, layer + 1))
                if layer == 1:
                    dve.wait_ge(affine, nth(affine, f, 1))
                    dve.tensor_tensor(fn_lo[:, :, :], c2, fn_hi[:, :, :].bitcast(F32), ALU.subtract
                                      ).then_inc(fn_lo_done, 1)
                else:
                    dve.wait_ge(normed, nth(normed, f, 1 if layer == 0 else 4))
                    dve.scalar_tensor_tensor(fn_lo[:, :, :], c1, 0.0, fn_hi[:, :, :].bitcast(F32),
                                             ALU.max, ALU.subtract).then_inc(fn_lo_done, 1)

            def edge(f, t):
                count = held(dve, nth(adj_in[t % 2], f, 16 * (t // 2 + 1)))
                dve.wait_ge(setup_done, 1)
                dve.wait_ge(adj_in[t % 2], count)
                count = held(dve, nth(edges_taken, f, 0))
                dve.wait_ge(setup_done, 1)
                dve.wait_ge(edges_taken, count)
                dve.tensor_scalar(edges_next[:, t, :], adj_rows[:, t % 2, :], 0.0, None, ALU.not_equal,
                                  saturate=False).then_inc(edges_done, 1)

            def adj_lo(f, t, q):
                js, ns = slice(4 * q, 4 * q + 4), slice(t * P, (t + 1) * P)
                dve.wait_ge(adj_hi_done, nth(adj_hi_done, f, 2 * t + q + 1))
                dve.tensor_tensor(adjT_lo[:, js, ns],
                                  P_F[q][:, :].rearrange("p (j n) -> p j n", j=4),
                                  adjT_hi[:, js, ns].bitcast(F32), ALU.subtract
                                  ).then_inc(adj_lo_done, 1)

            def eps_h(f, c):
                dve.wait_ge(fn_turned, nth(fn_turned, f, c + 1))
                dve.tensor_scalar(ehT[:, c * CH:(c + 1) * CH], P_F[c][:, :], 0.0, col(EPSC),
                                  ALU.max, ALU.mult).then_inc(ehT_done, 1)

            def agg_sum(f, c):
                cs = slice(c * CH, (c + 1) * CH)
                dve.wait_ge(ag_done, nth(ag_done, f, c + 1))
                dve.tensor_tensor(ehT[:, cs], P_F[c][:, :], ehT[:, cs], ALU.add
                                  ).then_inc(ag_summed, 1)

            def agg_lo(f, layer, c):
                cs = slice(c * CH, (c + 1) * CH)
                src = ehT[:, cs] if layer == 0 else P_F[c][:, :]
                dve.wait_ge(ag_hi_done, nth(ag_hi_done, f, 2 * layer + c + 1))
                dve.tensor_tensor(ag_lo[:, cs], src, ag_hi[:, cs].bitcast(F32), ALU.subtract
                                  ).then_inc(ag_lo_done, 1)

            def mlp1_bias(f, t):
                dve.wait_ge(hid_done, nth(hid_done, f, t + 1))
                dve.wait_ge(hid_turned, nth(hid_turned, f, t - 3))
                dve.tensor_tensor(hid[:, t % 4, :], P_F[0][:, :], b1_b[:, :], ALU.add
                                  ).then_inc(hid_biased, 1)

            def mean_square(f, v):
                dve.wait_ge(squared, nth(squared, f, 2 * v + 2))
                dve.tensor_scalar(mseps[:, 2 * v:2 * v + 2], ssq[:, 2 * v:2 * v + 2], 1.0 / H,
                                  EPS_RMS, ALU.mult, ALU.add).then_inc(mseps_done, 1)

            def rms_norm(f, t):
                dve.wait_ge(rrms_done, nth(rrms_done, f, t // 2 + 1))
                dve.scalar_tensor_tensor(hid[:, t % 4, :], hid[:, t % 4, :], rrms[:, t:t + 1],
                                         rms_b[:, :], ALU.mult, ALU.mult).then_inc(hid_normed, 1)

            def hidT_lo(f, t):
                bs = slice((t % 2) * P, (t % 2 + 1) * P)
                dve.wait_ge(hidT_hi_done, nth(hidT_hi_done, f, t + 1))
                dve.tensor_tensor(
                    y_lo[:, :].rearrange("p (b n) -> p b n", b=HB)[:, :, bs],
                    P_F[1][:, :].rearrange("p (b n) -> p b n", b=HB),
                    y_hi[:, :].bitcast(F32).rearrange("p (b n) -> p b n", b=HB)[:, :, bs],
                    ALU.subtract).then_inc(hidT_lo_done, 1)

            def x1(f, v):
                part = xf[:, 2 * v:2 * v + 2, :]
                dve.wait_ge(mlp_turned, nth(mlp_turned, f, v + 1))
                dve.tensor_tensor(part, P_F[1][:, 0:2 * P].rearrange("p (t d) -> p t d", d=D),
                                  part, ALU.add).then_inc(x1_done, 1)

            def hT_lo(f, c):
                cs = slice(c * CH, (c + 1) * CH)
                dve.wait_ge(hT_hi_done, nth(hT_hi_done, f, c + 1))
                dve.tensor_tensor(y_lo[:, cs], P_F[c][:, :], y_hi[:, cs].bitcast(F32), ALU.subtract
                                  ).then_inc(hT_lo_done, 1)

            def conv_add(f, layer, c):
                ts = slice(c * TC, (c + 1) * TC)
                dve.wait_ge(conv_turned, nth(conv_turned, f, 2 * layer - 2 + c + 1))
                src = P_F[c][:, :].rearrange("p (t d) -> p t d", d=D)
                if layer == 1:
                    dve.wait_ge(skip_added, nth(skip_added, f, 1))
                    dve.tensor_tensor(xf[:, ts, :], src, xf[:, ts, :], ALU.add
                                      ).then_inc(x2_done, 1)
                else:
                    dve.wait_ge(out_stored, nth(out_stored, f, 0))
                    dve.tensor_tensor(xg[:, ts, :], src, xf[:, ts, :], ALU.add
                                      ).then_inc(x3_done, 1)

            def take_edges(f):
                dve.wait_ge(s_done, nth(s_done, f, 0))
                dve.wait_ge(edges_done, nth(edges_done, f, KT))
                dve.tensor_copy(edges[:, :, :].bitcast(U16), edges_next[:, :, :].bitcast(U16)
                                ).then_inc(edges_taken, 1)

            def h0_nodes_lo(f, c):
                ts = slice(c * TC, (c + 1) * TC)
                dve.wait_ge(gn_hi_done, nth(gn_hi_done, f, c + 1))
                dve.tensor_tensor(gn_lo[:, ts, :], c1[:, ts, :], gn_hi[:, ts, :], ALU.subtract
                                  ).then_inc(gn_lo_done, 1)

            def arrived_lo(g, s, c):
                cs = slice(c * CH, (c + 1) * CH)
                dve.wait_ge(s_hi_done, nth(s_hi_done, g, 2 * s + c + 1))
                dve.scalar_tensor_tensor(s_lo[:, cs], P_S[c][:, :], 1.0 / HSCALE,
                                         s_hi[:, cs].bitcast(F32), ALU.mult, ALU.subtract
                                         ).then_inc(s_lo_done, 1)

            def r_times_hn(g, s, c):
                i = 2 * s + c
                dve.wait_ge(gate_done, nth(gate_done, g, 4 * i + 1))
                dve.wait_ge(rz_done, nth(rz_done, g, 2 * i + 1))
                dve.scalar_tensor_tensor(n_t[:, c, :], P_HN[:, :], col(BHN), r_t[:, c, :],
                                         ALU.add, ALU.mult).then_inc(rhn_done, 1)

            def n_arg(g, s, c):
                i = 2 * s + c
                dve.wait_ge(gate_done, nth(gate_done, g, 4 * i + 4))
                dve.wait_ge(rhn_done, nth(rhn_done, g, i + 1))
                dve.tensor_tensor(n_t[:, c, :], P_IN[:, :], n_t[:, c, :], ALU.add).then_inc(narg_done, 1)

            def new_part(g, s, c):
                i = 2 * s + c
                dve.wait_ge(n_done, nth(n_done, g, i + 1))
                dve.wait_ge(keep_done, nth(keep_done, g, i + 1))
                dve.tensor_tensor(n_t[:, c, :], n_t[:, c, :], r_t[:, c, :], ALU.mult
                                  ).then_inc(new_part_done, 1)

            def new_state(g, s, c):
                i = 2 * s + c
                cs = slice(c * CH, (c + 1) * CH)
                dve.wait_ge(new_part_done, nth(new_part_done, g, i + 1))
                dve.wait_ge(old_part_done, nth(old_part_done, g, i + 1))
                dve.tensor_tensor(h[:, cs], n_t[:, c, :], z_t[:, c, :], ALU.add).then_inc(h_new, 1)

            def nodes_lo(g, s, c):
                ts = slice(c * TC, (c + 1) * TC)
                if s < L - 1:
                    dve.wait_ge(gn_hi_done, nth(gn_hi_done, g, 2 * (s + 1) + c + 1))
                    dve.scalar_tensor_tensor(gn_lo[:, ts, :],
                                             P_T[c][:, :].rearrange("p (t d) -> p t d", d=D), HSCALE,
                                             gn_hi[:, ts, :], ALU.mult, ALU.subtract
                                             ).then_inc(gn_lo_done, 1)
                else:
                    dve.wait_ge(h_turned, nth(h_turned, g, 2 * s + c + 1))
                    dve.wait_ge(mask_in, nth(mask_in, g, 16))
                    for j in range(TC):
                        t = c * TC + j
                        last = dve.scalar_tensor_tensor(xg[:, t, :], P_T[c][:, j * P:(j + 1) * P],
                                                        mask[:, t:t + 1], xg[:, t, :],
                                                        ALU.mult, ALU.add)
                    last.then_inc(out_done, 1)

            dve.memset(neghalf[:, :], -0.5).then_inc(ident_done, 1)
            dve.memset(ssq[:, :], 0.0).then_inc(setup_done, 1)

            def split_weights():
                dve.wait_ge(w_loaded, N_WLOADS)
                dve.tensor_tensor(cols[:, BR:BR + 2], cols[:, BIR:BIR + 2], cols[:, BHR:BHR + 2], ALU.add
                                  ).then_inc(bias_done, 1)
                dve.wait_ge(bias_done, 1)
                dve.tensor_scalar(col(NEG_BZ), col(BZ), -1.0, None, ALU.mult).then_inc(bias_done, 1)
                dve.wait_ge(w_hi_done, 1)
                dve.tensor_tensor(w_lo[:, 0:NB], raw[:, 0:NB], w_hi[:, 0:NB].bitcast(F32), ALU.subtract
                                  ).then_inc(w_lo_done, 1)
                for l in range(L):
                    part = slice(O_G + l * G3, O_G + (l + 1) * G3)
                    dve.wait_ge(w_hi_done, l + 2)
                    dve.tensor_tensor(w_lo[:, part], bank[l][:, 0:G3], w_hi[:, part].bitcast(F32),
                                      ALU.subtract).then_inc(w_lo_done, 1)

            run(dve, DVE_ORDER, {
                "stats": norm_stats, "var": norm_var, "norm": norm_apply, "affine": affine_apply,
                "input": input_lo, "edge": edge, "adj": adj_lo, "turn0": eps_h,
                "sum": agg_sum, "gather": agg_lo, "mlp1": mlp1_bias, "msq": mean_square,
                "rms": rms_norm, "hidT": hidT_lo, "mlpT": x1, "turn1": hT_lo, "convT": conv_add,
                "edges": take_edges, "h0n": h0_nodes_lo, "agg": arrived_lo, "rhn": r_times_hn,
                "narg": n_arg, "zn": new_part, "h": new_state, "hT": nodes_lo},
                split_weights)

        @block.gpsimd
        def _(pool):
            def norm_power(f, j):
                pool.wait_ge(vareps_done, nth(vareps_done, f, j + 1))
                pool.wait_ge(normed, nth(normed, f, j))
                if j == 3:
                    pool.wait_ge(affine, nth(affine, f, 1))
                pool.tensor_tensor(rstd[:, :], vareps[:, :], neghalf[:, :], ALU.pow
                                   ).then_inc(rstd_done, 1)

            def add_skip(f):
                pool.wait_ge(relud, nth(relud, f, 1))
                pool.tensor_tensor(xf[:, :, :], xf[:, :, :], c1, ALU.add).then_inc(skip_added, 1)

            def rms_power(f, v):
                pool.wait_ge(mseps_done, nth(mseps_done, f, v + 1))
                pool.tensor_tensor(rrms[:, 2 * v:2 * v + 2], mseps[:, 2 * v:2 * v + 2],
                                   neghalf[:, 0:2], ALU.pow).then_inc(rrms_done, 1)

            def silu(f, t):
                pool.wait_ge(sig_done, nth(sig_done, f, t + 1))
                pool.tensor_tensor(hid[:, t % 4, :], hid[:, t % 4, :], sig[:, t % 2, :],
                                   ALU.mult).then_inc(silu_done, 1)

            def old_part(g, s, c):
                cs = slice(c * CH, (c + 1) * CH)
                pool.wait_ge(rz_done, nth(rz_done, g, 2 * (2 * s + c) + 2))
                pool.tensor_tensor(z_t[:, c, :], z_t[:, c, :], h[:, cs], ALU.mult
                                   ).then_inc(old_part_done, 1)

            def split_state(g, s, c):
                cs = slice(c * CH, (c + 1) * CH)
                count = held(pool, nth(h_new, g, 2 * s + c + 1))
                pool.wait_ge(setup_done, 1)
                pool.wait_ge(h_new, count)
                pool.tensor_scalar(h_hi[:, cs], h[:, cs], 1.0, 0.0, ALU.mult, ALU.add
                                   ).then_inc(h_hi_done, 1)
                pool.wait_ge(h_hi_done, nth(h_hi_done, g, 2 * s + c + 1))
                pool.tensor_tensor(h_lo[:, cs], h[:, cs], h_hi[:, cs].bitcast(F32), ALU.subtract
                                   ).then_inc(h_lo_done, 1)

            pool.memset(ident[:, :], 0.0).then_inc(ident_done, 1)
            pool.wait_ge(ident_done, 2)
            pool.affine_select(out=ident[:, :], in_=ident[:, :], compare_op=ALU.not_equal, fill=1.0,
                               base=0, pattern=[[-1, P]], channel_multiplier=1
                               ).then_inc(ident_done, 1)
            run(pool, POOL_ORDER, {"power": norm_power, "skip": add_skip, "rms": rms_power,
                                   "silu": silu, "split": split_state, "zh": old_part})


def kernel(**inputs):
    import numpy as _np
    import concourse.bacc as _bacc
    from concourse import mybir as _mybir
    from concourse.bass_utils import run_bass_kernel_spmd as _run

    c = _np.ascontiguousarray
    laid = {
        "x": c(inputs["x"]), "adj": c(inputs["adj"]), "nodemask": c(_np.transpose(inputs["nodemask"].reshape(8, 8, 128), (0, 2, 1))),
        "epsilon": c(inputs["L0_gnn_epsilon"]).reshape(1),
        "W1": c(inputs["L0_gnn_W1"]), "b1": c(inputs["L0_gnn_b1"]), "rms": c(inputs["L0_gnn_rms_weight"]),
        "W2": c(inputs["L0_gnn_W2"]), "b2": c(inputs["L0_gnn_b2"]),
        "W_rel": c(inputs["L1_gnn_W_rel"]), "b_rel": c(inputs["L1_gnn_b_rel"]),
        "W_root": c(inputs["L1_gnn_W_root"]), "gamma": c(inputs["L1_gnn_ln_gamma"]),
        "beta": c(inputs["L1_gnn_ln_beta"]),
        "W_l2": c(inputs["L2_gnn_weight"]), "b_l2": c(inputs["L2_gnn_bias"]),
        "WlT": c(_np.transpose(inputs["L3_gnn_weight"], (0, 2, 1))),
        "wihT": c(_np.transpose(inputs["L3_gnn_w_ih"])), "whhT": c(_np.transpose(inputs["L3_gnn_w_hh"])),
        "b_ih": c(_np.transpose(inputs["L3_gnn_b_ih"].reshape(3, 128))),
        "b_hh": c(_np.transpose(inputs["L3_gnn_b_hh"].reshape(3, 128))),
    }
    nc = _bacc.Bacc("TRN2", target_bir_lowering=False, num_devices=1)
    arrays, args = {}, {}
    for name, a in laid.items():
        arrays[f"in_{name}_dram"] = a
        args[name] = nc.dram_tensor(f"in_{name}_dram", a.shape, _mybir.dt.from_np(a.dtype),
                                    kind="ExternalInput").ap()
    out = nc.dram_tensor("out_0_dram", laid["x"].shape, _mybir.dt.from_np(laid["x"].dtype),
                         kind="ExternalOutput").ap()
    adj_preln_kernel(nc, args, out)
    r = _run(nc, [arrays], core_ids=[0])
    return r.results[0]["out_0_dram"]
```
